# Optimizing a Trainium2 kernel written in Bass

```python
import numpy as np
import jax
import jax.numpy as jnp

def _softmax(x, axis=-1):
    return jax.nn.softmax(x, axis=axis)

def _gelu(x):
    return jax.nn.gelu(x, approximate=True)

def _silu(x):
    return jax.nn.silu(x)

def _sigmoid(x):
    return jax.nn.sigmoid(x)

def _layernorm(x, axis=-1, eps=1e-05):
    m = jnp.mean(x, axis=axis, keepdims=True)
    v = jnp.var(x, axis=axis, keepdims=True)
    return (x - m) / jnp.sqrt(v + eps)

def _scatter_add(tgt, idx, src, axis=0):
    return tgt.at[idx].add(src)

def _segment_sum(src, seg, n):
    return jax.ops.segment_sum(src, seg, n)
kernel_name = 'mk_gnn_preln_d4_gnn_r64_4bbb54'

def setup_inputs(seed: int=0):
    np.random.seed(seed)
    _w = jnp.asarray

    def _rec_inputs():
        import jax
        import jax.numpy as jnp
        _gk = jax.random.key(seed)
        x = -0.0009044 + 1 * jax.random.normal(jax.random.fold_in(_gk, 1), (100000, 16), jnp.float32)
        src = jax.random.randint(jax.random.fold_in(_gk, 2), (50000,), 0, 100000, jnp.int32)
        dst = jax.random.randint(jax.random.fold_in(_gk, 3), (50000,), 0, 100000, jnp.int32)
        _o = jnp.argsort(dst, stable=True)
        src = src[_o]
        dst = dst[_o]
        edge_attr_16 = -0.00010739 + 0.99994 * jax.random.normal(jax.random.fold_in(_gk, 12), (50000, 16), jnp.float32)
        edge_type_8 = jax.random.randint(jax.random.fold_in(_gk, 14), (50000,), 0, 8, jnp.int32)
        edge_type_90 = jax.random.randint(jax.random.fold_in(_gk, 15), (50000,), 0, 90, jnp.int32)
        edge_weight = jax.random.uniform(jax.random.fold_in(_gk, 16), (50000,), jnp.float32, 0.0, 1)
        return (x, src, dst, edge_attr_16, edge_type_8, edge_type_90, edge_weight)
    x, src, dst, edge_attr_16, edge_type_8, edge_type_90, edge_weight = _rec_inputs()

    def _L0_gnn_setup():
        import jax, jax.numpy as jnp
        import numpy as np
        N = 100000
        E = 12500
        F_IN = 16
        H1, C1 = (3, 32)
        H2, C2 = (1, 32)
        NC = 16
        SLOPE = 0.2

        def _gat_layer(x, src, dst, W, a_s, a_d, b, heads, outc):
            h = (x @ W).reshape(N, heads, outc)
            alpha_s = (h * a_s).sum(-1)
            alpha_d = (h * a_d).sum(-1)
            e = jax.nn.leaky_relu(alpha_s[src] + alpha_d[dst], SLOPE)
            m = jax.ops.segment_max(e, dst, num_segments=N)
            p = jnp.exp(e - m[dst])
            z = jax.ops.segment_sum(p, dst, num_segments=N)
            alpha = p / (z[dst] + 1e-16)
            out = jax.ops.segment_sum(h[src] * alpha[:, :, None], dst, num_segments=N)
            return out.reshape(N, heads * outc) + b
        key = jax.random.key(seed)
        ks = jax.random.split(key, 12)
        s = 0.1
        return {'x': jax.random.normal(ks[0], (N, F_IN), jnp.float32), 'edge_index': jax.random.randint(ks[1], (2, E), 0, N, dtype=jnp.int32), 'W1': jax.random.normal(ks[2], (F_IN, H1 * C1), jnp.float32) * s, 'a_src1': jax.random.normal(ks[3], (H1, C1), jnp.float32) * s, 'a_dst1': jax.random.normal(ks[4], (H1, C1), jnp.float32) * s, 'b1': jnp.zeros((H1 * C1,), jnp.float32), 'W2': jax.random.normal(ks[5], (H1 * C1, H2 * C2), jnp.float32) * s, 'a_src2': jax.random.normal(ks[6], (H2, C2), jnp.float32) * s, 'a_dst2': jax.random.normal(ks[7], (H2, C2), jnp.float32) * s, 'b2': jnp.zeros((H2 * C2,), jnp.float32), 'Wf': jax.random.normal(ks[8], (C2, NC), jnp.float32) * s, 'bf': jnp.zeros((NC,), jnp.float32)}
    _L0_gnn_all = _L0_gnn_setup()
    _L0_gnn_in = {k: v for k, v in _L0_gnn_all.items() if k in ('W1', 'a_src1', 'a_dst1', 'b1', 'W2', 'a_src2', 'a_dst2', 'b2', 'Wf', 'bf')}
    del _L0_gnn_all

    def _L1_gnn_setup():
        import jax, jax.numpy as jnp
        import numpy as np
        N_NODES = 100000
        N_EDGES = 50000
        NUM_REL = 8

        def _rgcn_layer(x, src, dst, edge_type, W, root, bias):
            out = x @ root + bias
            x_src = x[src]
            for r in range(W.shape[0]):
                mask = (edge_type == r).astype(x.dtype)
                s = jax.ops.segment_sum(x_src * mask[:, None], dst, num_segments=x.shape[0])
                cnt = jax.ops.segment_sum(mask, dst, num_segments=x.shape[0])
                agg = s / jnp.clip(cnt, 1.0)[:, None]
                out = out + agg @ W[r]
            return out
        key = jax.random.key(seed)
        ks = jax.random.split(key, 9)
        x = jax.random.normal(ks[0], (N_NODES, 16), dtype=jnp.float32)
        edge_index = jax.random.randint(ks[1], (2, N_EDGES), 0, N_NODES, dtype=jnp.int32)
        edge_type = jax.random.randint(ks[2], (N_EDGES,), 0, NUM_REL, dtype=jnp.int32)
        s1 = 1.0 / np.sqrt(16.0)
        s2 = 1.0 / np.sqrt(32.0)
        W1 = jax.random.normal(ks[3], (NUM_REL, 16, 32), dtype=jnp.float32) * s1
        root1 = jax.random.normal(ks[4], (16, 32), dtype=jnp.float32) * s1
        b1 = jnp.zeros((32,), dtype=jnp.float32)
        W2 = jax.random.normal(ks[5], (NUM_REL, 32, 16), dtype=jnp.float32) * s2
        root2 = jax.random.normal(ks[6], (32, 16), dtype=jnp.float32) * s2
        b2 = jnp.zeros((16,), dtype=jnp.float32)
        return {'x': x, 'edge_index': edge_index, 'edge_type': edge_type, 'W1': W1, 'root1': root1, 'b1': b1, 'W2': W2, 'root2': root2, 'b2': b2}
    _L1_gnn_all = _L1_gnn_setup()
    _L1_gnn_in = {k: v for k, v in _L1_gnn_all.items() if k in ('W1', 'root1', 'b1', 'W2', 'root2', 'b2')}
    del _L1_gnn_all

    def _L2_gnn_setup():
        import jax, jax.numpy as jnp
        import numpy as np
        N_NODES = 100000
        N_EDGES = 50000
        DIM = 16
        B, K, C, D, E, H = (0.1, 5.0, 1.0, 5.0, 0.9, 0.1)
        E_ = E
        key = jax.random.key(seed)
        k1, k2, k3, k4 = jax.random.split(key, 4)
        x = jax.random.uniform(k1, (N_NODES, DIM), dtype=jnp.float32)
        edge_src = jax.random.randint(k2, (N_EDGES,), 0, N_NODES, dtype=jnp.int32)
        edge_dst = jax.random.randint(k3, (N_EDGES,), 0, N_NODES, dtype=jnp.int32)
        edge_vals = jax.random.uniform(k4, (N_EDGES,), dtype=jnp.float32)
        return {'x': x, 'edge_src': edge_src, 'edge_dst': edge_dst, 'edge_vals': edge_vals}
    _L2_gnn_all = _L2_gnn_setup()
    _L2_gnn_in = {k: v for k, v in _L2_gnn_all.items() if k in ()}
    del _L2_gnn_all

    def _L3_gnn_setup():
        import jax, jax.numpy as jnp
        import numpy as np
        N, E, IN, OUT, R, B = (50000, 12500, 16, 16, 90, 30)
        key = jax.random.key(seed)
        ks = jax.random.split(key, 9)
        h = jax.random.normal(ks[0], (N, IN), dtype=jnp.float32)
        he = jax.random.normal(ks[1], (E, IN), dtype=jnp.float32)
        Ws = jax.random.normal(ks[2], (OUT, IN), dtype=jnp.float32) * 0.1
        Wa = jax.random.normal(ks[3], (1, 3 * OUT), dtype=jnp.float32) * 0.1
        weight = jax.random.normal(ks[4], (B, IN, OUT), dtype=jnp.float32) * 0.1
        w_comp = jax.random.normal(ks[5], (R, B), dtype=jnp.float32) * 0.1
        src = jax.random.randint(ks[6], (E,), 0, N)
        dst = jax.random.randint(ks[7], (E,), 0, N)
        rel_type = jax.random.randint(ks[8], (E,), 0, R)
        return {'h': h, 'he': he, 'Ws': Ws, 'Wa': Wa, 'weight': weight, 'w_comp': w_comp, 'src': src, 'dst': dst, 'rel_type': rel_type}
    _L3_gnn_all = _L3_gnn_setup()
    _L3_gnn_in = {k: v for k, v in _L3_gnn_all.items() if k in ('Ws', 'Wa', 'weight', 'w_comp')}
    del _L3_gnn_all
    return {'x': x, 'src': src, 'dst': dst, 'edge_attr_16': edge_attr_16, 'edge_type_8': edge_type_8, 'edge_type_90': edge_type_90, 'edge_weight': edge_weight, 'L0_gnn_W1': _L0_gnn_in['W1'], 'L0_gnn_a_src1': _L0_gnn_in['a_src1'], 'L0_gnn_a_dst1': _L0_gnn_in['a_dst1'], 'L0_gnn_b1': _L0_gnn_in['b1'], 'L0_gnn_W2': _L0_gnn_in['W2'], 'L0_gnn_a_src2': _L0_gnn_in['a_src2'], 'L0_gnn_a_dst2': _L0_gnn_in['a_dst2'], 'L0_gnn_b2': _L0_gnn_in['b2'], 'L0_gnn_Wf': _L0_gnn_in['Wf'], 'L0_gnn_bf': _L0_gnn_in['bf'], 'L1_gnn_W1': _L1_gnn_in['W1'], 'L1_gnn_root1': _L1_gnn_in['root1'], 'L1_gnn_b1': _L1_gnn_in['b1'], 'L1_gnn_W2': _L1_gnn_in['W2'], 'L1_gnn_root2': _L1_gnn_in['root2'], 'L1_gnn_b2': _L1_gnn_in['b2'], 'L3_gnn_Ws': _L3_gnn_in['Ws'], 'L3_gnn_Wa': _L3_gnn_in['Wa'], 'L3_gnn_weight': _L3_gnn_in['weight'], 'L3_gnn_w_comp': _L3_gnn_in['w_comp']}

def reference(x, src, dst, edge_attr_16, edge_type_8, edge_type_90, edge_weight, L0_gnn_W1, L0_gnn_a_src1, L0_gnn_a_dst1, L0_gnn_b1, L0_gnn_W2, L0_gnn_a_src2, L0_gnn_a_dst2, L0_gnn_b2, L0_gnn_Wf, L0_gnn_bf, L1_gnn_W1, L1_gnn_root1, L1_gnn_b1, L1_gnn_W2, L1_gnn_root2, L1_gnn_b2, L3_gnn_Ws, L3_gnn_Wa, L3_gnn_weight, L3_gnn_w_comp):
    import jax
    import jax.numpy as jnp

    def _L0_gnn_ref(x, edge_index, W1, a_src1, a_dst1, b1, W2, a_src2, a_dst2, b2, Wf, bf):
        import jax, jax.numpy as jnp
        import numpy as np
        N = 100000
        E = 12500
        F_IN = 16
        H1, C1 = (3, 32)
        H2, C2 = (1, 32)
        NC = 16
        SLOPE = 0.2

        def _gat_layer(x, src, dst, W, a_s, a_d, b, heads, outc):
            h = (x @ W).reshape(N, heads, outc)
            alpha_s = (h * a_s).sum(-1)
            alpha_d = (h * a_d).sum(-1)
            e = jax.nn.leaky_relu(alpha_s[src] + alpha_d[dst], SLOPE)
            m = jax.ops.segment_max(e, dst, num_segments=N)
            p = jnp.exp(e - m[dst])
            z = jax.ops.segment_sum(p, dst, num_segments=N)
            alpha = p / (z[dst] + 1e-16)
            out = jax.ops.segment_sum(h[src] * alpha[:, :, None], dst, num_segments=N)
            return out.reshape(N, heads * outc) + b
        loops = jnp.arange(N, dtype=edge_index.dtype)
        src = jnp.concatenate([edge_index[0], loops])
        dst = jnp.concatenate([edge_index[1], loops])
        h = jax.nn.selu(_gat_layer(x, src, dst, W1, a_src1, a_dst1, b1, H1, C1))
        h = jax.nn.selu(_gat_layer(h, src, dst, W2, a_src2, a_dst2, b2, H2, C2))
        return h @ Wf + bf

    def _L1_gnn_ref(x, edge_index, edge_type, W1, root1, b1, W2, root2, b2):
        import jax, jax.numpy as jnp
        import numpy as np
        N_NODES = 100000
        N_EDGES = 50000
        NUM_REL = 8

        def _rgcn_layer(x, src, dst, edge_type, W, root, bias):
            out = x @ root + bias
            x_src = x[src]
            for r in range(W.shape[0]):
                mask = (edge_type == r).astype(x.dtype)
                s = jax.ops.segment_sum(x_src * mask[:, None], dst, num_segments=x.shape[0])
                cnt = jax.ops.segment_sum(mask, dst, num_segments=x.shape[0])
                agg = s / jnp.clip(cnt, 1.0)[:, None]
                out = out + agg @ W[r]
            return out
        src, dst = (edge_index[0], edge_index[1])
        h = _rgcn_layer(x, src, dst, edge_type, W1, root1, b1)
        h = jax.nn.relu(h)
        h = _rgcn_layer(h, src, dst, edge_type, W2, root2, b2)
        return h

    def _L2_gnn_ref(x, edge_src, edge_dst, edge_vals):
        import jax, jax.numpy as jnp
        import numpy as np
        N_NODES = 100000
        N_EDGES = 50000
        DIM = 16
        B, K, C, D, E, H = (0.1, 5.0, 1.0, 5.0, 0.9, 0.1)
        E_ = E
        n = x.shape[0]
        f = B + x * (1.0 - x / K) * (x / C - 1.0)
        xi = x[edge_src]
        xj = x[edge_dst]
        msg = edge_vals[:, None] * xi * xj / (D + E_ * xi + H * xj)
        f = f + jax.ops.segment_sum(msg, edge_src, num_segments=n)
        return f

    def _L3_gnn_ref(h, he, Ws, Wa, weight, w_comp, src, dst, rel_type):
        import jax, jax.numpy as jnp
        import numpy as np
        N, E, IN, OUT, R, B = (50000, 12500, 16, 16, 90, 30)
        n_nodes, in_dim = h.shape
        num_bases, _, out_dim = weight.shape
        num_rels = w_comp.shape[0]
        V = weight.reshape(in_dim, num_bases, out_dim)
        W_rel = jnp.matmul(w_comp, V).reshape(num_rels, in_dim, out_dim)
        h_src = h[src]
        z_src = h_src @ Ws.T
        z_dst = h[dst] @ Ws.T
        z_e = he @ Ws.T
        e = jnp.concatenate([z_src, z_e, z_dst], axis=1) @ Wa.T
        msg = jnp.einsum('ei,eio->eo', h_src, W_rel[rel_type]) * e
        h_out = jax.ops.segment_sum(msg, dst, num_segments=n_nodes)
        return h_out
    edge_index = jnp.stack([src, dst])
    h = jnp.maximum(_layernorm(x, axis=-1), 0.0)
    x = x + _L0_gnn_ref(h, edge_index, L0_gnn_W1, L0_gnn_a_src1, L0_gnn_a_dst1, L0_gnn_b1, L0_gnn_W2, L0_gnn_a_src2, L0_gnn_a_dst2, L0_gnn_b2, L0_gnn_Wf, L0_gnn_bf)
    h = jnp.maximum(_layernorm(x, axis=-1), 0.0)
    x = x + _L1_gnn_ref(h, edge_index, edge_type_8, L1_gnn_W1, L1_gnn_root1, L1_gnn_b1, L1_gnn_W2, L1_gnn_root2, L1_gnn_b2)
    h = jnp.maximum(_layernorm(x, axis=-1), 0.0)
    x = x + _L2_gnn_ref(h, src, dst, edge_weight)
    h = jnp.maximum(_layernorm(x, axis=-1), 0.0)
    x = x + _L3_gnn_ref(h, edge_attr_16, L3_gnn_Ws, L3_gnn_Wa, L3_gnn_weight, L3_gnn_w_comp, src, dst, edge_type_90)
    return x

_drawn_inputs = setup_inputs


def setup_inputs(seed=0):
    import zlib

    import numpy as np

    out = dict(_drawn_inputs(seed))
    spreads = {'L0_gnn_b1': (0.0, 0.1),
     'L0_gnn_b2': (0.0, 0.1),
     'L0_gnn_bf': (0.0, 0.1),
     'L1_gnn_b1': (0.0, 0.1),
     'L1_gnn_b2': (0.0, 0.1)}
    factors = {'edge_attr_16': 3.329,
     'edge_weight': 4.481,
     'L0_gnn_a_src1': 22.42,
     'L0_gnn_a_dst1': 52.15,
     'L0_gnn_a_src2': 24.536,
     'L0_gnn_a_dst2': 64.0,
     'L3_gnn_Wa': 2.888}
    for name, (base, spread) in spreads.items():
        noise = np.random.default_rng([zlib.crc32(name.encode()), seed]).standard_normal(out[name].shape)
        drawn = base * np.exp(spread * noise) if base else spread * noise
        out[name] = jnp.asarray(drawn.astype(out[name].dtype))
    for name, factor in factors.items():
        out[name] = (out[name] * factor).astype(out[name].dtype)
    return out
```

```python
from contextlib import ExitStack

import concourse.bass as bass
from concourse import mybir

ALU = mybir.AluOpType
ACT = mybir.ActivationFunctionType
F32 = mybir.dt.float32
I32 = mybir.dt.int32
AX_X = mybir.AxisListType.X

P = 128
FEAT = 16
HEADS1, CH = 3, 32
HID = HEADS1 * CH
NREL, RELS, BASES = 8, 90, 30

B = 7
C = 800

SLOPE = 0.2
EPS = 1e-5
SELU_ALPHA = 1.6732632423543772
SELU_SCALE = 1.0507009873554805
FAR = -1e30
WIDTH1 = HEADS1 * FEAT + HEADS1 + NREL
WIDTH2 = CH + 1


class Steps:

    def __init__(self, engine, sem, base=0, apart=False):
        self.engine, self.sem, self.base, self.n, self.apart = engine, sem, base, 0, apart

    def link(self, instruction):
        self.n += 1
        instruction.then_inc(self.sem, 1)
        self.engine.wait_ge(self.sem, self.base + self.n)
        if self.apart:
            self.engine.nop(nofuse=True)


def hold(engine, sem, value):
    engine.wait_ge(sem, value)
    engine.nop(nofuse=True)


def bcast(ap, shape):
    return ap.broadcast_to(shape)


def gnn_kernel(nc, x, src, dst, edge_attr_16, edge_type_8, edge_type_90, edge_weight,
               W1, a_src1, a_dst1, b1, W2, a_src2, a_dst2, b2, Wf, bf,
               RW1, root1, rb1, RW2, root2, rb2, Ws, Wa, bases, w_comp, out):
    N = x.shape[0]
    E = src.shape[0]
    T = -(-E // (P * 2 * B)) * 2 * B
    ITER = T // (2 * B)
    EP = E // T
    EREST = E - EP * T
    NPART = N // C
    NP = P * C
    assert EP == P - 1 and NPART * C == N and NP - N >= P
    AHEAD = 2 * B

    def scratch(name, shape, dt=F32):
        return nc.dram_tensor(name, shape, dt, kind="Internal").ap()

    t_gat1 = scratch("t_gat1", (NP, FEAT + HEADS1))
    t_norm1 = scratch("t_norm1", (NP, 2 * HEADS1))
    t_gat2 = scratch("t_gat2", (NP, CH + 1))
    t_norm2 = scratch("t_norm2", (NP, 2 + NREL))
    t_rel1 = scratch("t_rel1", (NP, FEAT))
    t_rel2 = scratch("t_rel2", (NP, CH))
    t_mix = scratch("t_mix", (NP, FEAT))
    t_last = scratch("t_last", (NP, FEAT))
    max1 = [scratch(f"max1_{s}", (NP, HEADS1)) for s in range(B)]
    max2 = [scratch(f"max2_{s}", (NP, 1)) for s in range(B)]
    acc1 = [scratch(f"acc1_{r}", (NP, WIDTH1)) for r in range(2)]
    acc2 = [scratch(f"acc2_{r}", (NP, WIDTH2)) for r in range(2)]
    acc3 = [scratch(f"acc3_{r}", (NP, CH)) for r in range(2)]
    acc4 = [scratch(f"acc4_{r}", (NP, FEAT)) for r in range(2)]
    acc5 = [scratch(f"acc5_{r}", (NP, FEAT)) for r in range(2)]
    acc6 = [scratch(f"acc6_{r}", (NP, 2 * FEAT)) for r in range(2)]
    row_src = scratch("row_src", (T, P))
    row_dst = scratch("row_dst", (T, P))
    row_typ = scratch("row_typ", (T, P))
    w_rel_dram = scratch("w_rel_dram", (RELS * FEAT, FEAT))
    primer = scratch("primer", (P, 4))

    def by_node(table):
        return table.rearrange("(p c) f -> p c f", p=P)

    def flat(table):
        return table.rearrange("(p c) f -> p (c f)", p=P)

    in_phase = {}

    def semaphore(ctx, name):
        if id(ctx) not in in_phase:
            in_phase[id(ctx)] = []
            ctx.callback(clear, id(ctx))
        in_phase[id(ctx)].append(nc.alloc_semaphore(name))
        return in_phase[id(ctx)][-1]

    def clear(phase):
        nc.clear_and_free_semaphores(in_phase.pop(phase))
        nc.all_engine_barrier()

    with ExitStack() as top:
        def sb(name, shape, dt=F32, ctx=top):
            return ctx.enter_context(nc.sbuf_tensor(name, shape, dt))

        X = sb("X", [P, C, FEAT])
        src_i = sb("src_i", [P, T + AHEAD], I32)
        dst_i = sb("dst_i", [P, T + AHEAD], I32)
        src_f = sb("src_f", [P, T])
        dst_f = sb("dst_f", [P, T])
        rel_f = sb("rel_f", [P, T])
        weight = sb("weight", [P, T])
        inv_cnt = sb("inv_cnt", [P, T])
        uniq_dst = sb("uniq_dst", [P, T], I32)
        uniq_src = sb("uniq_src", [P, T], I32)
        ident = sb("ident", [P, P])
        earlier = sb("earlier", [P, P])
        iota8 = sb("iota8", [P, NREL])
        lane = sb("lane", [P, 1])
        spare = sb("spare", [P, 1])
        bd_score = sb("bd_score", [P, 8, 2 * HEADS1])
        w1_half = sb("w1_half", [HID, 2, HEADS1, CH])
        b1_col = sb("b1_col", [HID, 2])
        w2_ext = sb("w2_ext", [HID, CH + 2])
        w2_const = sb("w2_const", [P, CH + 2])
        bd_wf = sb("bd_wf", [P, 4, FEAT])
        wf_const = sb("wf_const", [P, FEAT])
        b2_row = sb("b2_row", [P, CH])
        rel_w1 = sb("rel_w1", [P, CH])
        rel_w2 = sb("rel_w2", [P, 2, FEAT])
        bd_root1 = sb("bd_root1", [P, 8, CH])
        bd_root2 = sb("bd_root2", [P, 4, FEAT])
        rb1_row = sb("rb1_row", [P, CH])
        rb2_row = sb("rb2_row", [P, FEAT])
        c_row = sb("c_row", [P, 3, FEAT])
        w_rel = sb("w_rel", [P, FEAT, FEAT])
        primed = sb("primed", [P, 4])

        def psum_all(ctx, name):
            return ctx.enter_context(nc.psum_tensor(name, [P, 8 * 512], F32))

        with ExitStack() as ctx:
            def tmp(name, shape, dt=F32):
                return sb(name, shape, dt, ctx)

            def sem(name):
                return semaphore(ctx, name)

            rel_i = tmp("rel_i", [P, T], I32)
            typ_i = tmp("typ_i", [P, T], I32)
            typ_f = tmp("typ_f", [P, T])
            w1_rep = tmp("w1_rep", [P, HID])
            a1_rep = tmp("a1_rep", [P, 2, HID])
            prod1 = tmp("prod1", [P, 2, HID])
            score1 = tmp("score1", [P, 2 * HEADS1])
            w2_raw = tmp("w2_raw", [HID, CH])
            a2_rep = tmp("a2_rep", [HID, 2, CH])
            prod2 = tmp("prod2", [HID, 2, CH])
            wf_rep = tmp("wf_rep", [P, FEAT])
            bf_row = tmp("bf_row", [P, FEAT])
            root1_rep = tmp("root1_rep", [P, CH])
            root2_rep = tmp("root2_rep", [P, FEAT])
            mask8 = tmp("mask8", [P, 8])
            mask4 = tmp("mask4", [P, 4])
            ones = tmp("ones", [P, P])
            ws_sb = tmp("ws_sb", [FEAT, FEAT])
            wa_sb = tmp("wa_sb", [FEAT, 3])
            wa_wide = tmp("wa_wide", [FEAT, 3, P])
            basis = tmp("basis", [BASES, FEAT, FEAT])
            comp_t = tmp("comp_t", [BASES, RELS])
            w_flat = tmp("w_flat", [RELS, FEAT, FEAT])
            QT = T // 4
            rows = tmp("rows", [QT, 3, 4, P])
            ps = psum_all(ctx, "ps_setup")
            s_cleared = sem("s_cleared")
            s_masks = sem("s_masks")
            s_loaded = sem("s_loaded")
            s_float = sem("s_float")
            s_step = sem("s_step")
            s_rows_t = sem("s_rows_t")
            s_rows = sem("s_rows")
            s_wts = sem("s_wts")
            s_prods = sem("s_prods")
            s_flat = sem("s_flat")
            s_stored = sem("s_stored")
            s_back = sem("s_back")
            n_loads = [0]
            with nc.Block() as block:
                @block.sync
                def _(sp):
                    def load(to, frm):
                        sp.dma_start(to, frm).then_inc(s_loaded, 16)
                        n_loads[0] += 1

                    sp.wait_ge(s_cleared, 1)
                    for to, frm in ((src_i, src), (dst_i, dst), (rel_i, edge_type_8), (typ_i, edge_type_90),
                                    (weight, edge_weight)):
                        load(to[0:EP, 0:T], frm[0:EP * T].rearrange("(p t) -> p t", t=T))
                        load(to[EP:EP + 1, 0:EREST], frm[EP * T:E].rearrange("(p t) -> p t", p=1))
                    for j in range(8):
                        load(w1_rep[FEAT * j:FEAT * (j + 1), :], W1)
                        load(root1_rep[FEAT * j:FEAT * (j + 1), :], root1)
                    for j in range(4):
                        load(wf_rep[CH * j:CH * (j + 1), :], Wf)
                        load(root2_rep[CH * j:CH * (j + 1), :], root2)
                    load(a1_rep[:, 0, :], a_src1.rearrange("h c -> (h c)").partition_broadcast(P))
                    load(a1_rep[:, 1, :], a_dst1.rearrange("h c -> (h c)").partition_broadcast(P))
                    load(a2_rep[:, 0, :], a_src2.rearrange("h c -> (h c)").partition_broadcast(HID))
                    load(a2_rep[:, 1, :], a_dst2.rearrange("h c -> (h c)").partition_broadcast(HID))
                    load(w2_raw[:], W2)
                    load(b1_col[:, 0:1], b1.rearrange("(c o) -> c o", o=1))
                    load(bf_row[:], bf.partition_broadcast(P))
                    load(b2_row[:], b2.partition_broadcast(P))
                    load(rb1_row[:], rb1.partition_broadcast(P))
                    load(rb2_row[:], rb2.partition_broadcast(P))
                    load(rel_w1[:], RW1.rearrange("r f c -> (r f) c"))
                    load(rel_w2[:], RW2.rearrange("(a r) f c -> (r f) a c", a=2))
                    load(ws_sb[:], Ws)
                    with nc.allow_non_contiguous_dma(reason="small transposed weights"):
                        load(wa_sb[:], Wa.rearrange("a (k o) -> o (a k)", k=3))
                        load(comp_t[:], w_comp.rearrange("r b -> b r"))
                    load(basis[:], bases.rearrange("b i o -> (b i o)").rearrange("(i b o) -> b i o", b=BASES, o=FEAT))
                    load(X[0:NPART, :, :], x.rearrange("(p c) f -> p c f", c=C))
                    sp.wait_ge(s_rows, 3)
                    for n, table in enumerate((row_src, row_dst, row_typ)):
                        sp.dma_start(table.rearrange("(k q) p -> q k p", q=QT), rows[:, n]).then_inc(s_stored, 16)
                    sp.wait_ge(s_flat, 1)
                    sp.dma_start(w_rel_dram.rearrange("(i r) o -> r i o", r=RELS), w_flat[:]).then_inc(s_stored, 16)
                    sp.wait_ge(s_stored, 64)
                    sp.dma_start(w_rel[0:RELS], w_rel_dram.rearrange("(r i) o -> r i o", i=FEAT)).then_inc(s_back, 16)
                    sp.wait_ge(s_back, 16)
                    sp.wait_ge(s_loaded, 16 * n_loads[0])

                n_in = 16 * (10 + 16 + 8 + 4 + 1 + 1 + 4 + 2 + 1 + 2 + 1 + 1)

                @block.gpsimd
                def _(pool):
                    step = Steps(pool, s_masks)
                    g = nc.gpsimd
                    step.link(g.memset(ident[:], 0.0))
                    step.link(g.affine_select(out=ident[:], in_=ident[:], compare_op=ALU.not_equal, fill=1.0, base=0,
                                              pattern=[[-1, P]], channel_multiplier=1))
                    step.link(g.memset(earlier[:], 1.0))
                    step.link(g.affine_select(out=earlier[:], in_=earlier[:], compare_op=ALU.is_ge, fill=0.0, base=-1,
                                              pattern=[[-1, P]], channel_multiplier=1))
                    step.link(g.memset(ones[:], 1.0))
                    for mask, n, w in ((mask8, 8, 16), (mask4, 4, 32)):
                        step.link(g.memset(mask[:], 1.0))
                        step.link(g.affine_select(out=mask[:], in_=mask[:], compare_op=ALU.is_ge, fill=0.0, base=0,
                                                  pattern=[[-w, n]], channel_multiplier=1))
                        step.link(g.affine_select(out=mask[:], in_=mask[:], compare_op=ALU.is_ge, fill=0.0,
                                                  base=w - 1, pattern=[[w, n]], channel_multiplier=-1))
                    step.link(g.iota(lane[:], pattern=[[0, 1]], base=0, channel_multiplier=1,
                                     allow_small_or_imprecise_dtypes=True))
                    step.link(g.iota(spare[:], pattern=[[0, 1]], base=N, channel_multiplier=1,
                                     allow_small_or_imprecise_dtypes=True))
                    step.link(g.iota(iota8[:], pattern=[[1, NREL]], base=0, channel_multiplier=0,
                                     allow_small_or_imprecise_dtypes=True))

                n_masks = 14

                @block.vector
                def _(dve):
                    v = nc.vector
                    step = Steps(dve, s_step)
                    v.memset(src_i[:], N + P - 1)
                    v.memset(dst_i[:], N + P - 1)
                    v.memset(rel_i[:], 0)
                    v.memset(typ_i[:], 0)
                    v.memset(weight[:], 0.0)
                    v.memset(w_rel[:], 0.0)
                    v.memset(primed[:], 0.0)
                    v.memset(X[96:P, :, :], 0.0).then_inc(s_cleared, 1)
                    dve.wait_ge(s_loaded, n_in)
                    v.tensor_copy(src_f[:], src_i[:, 0:T])
                    v.tensor_copy(dst_f[:], dst_i[:, 0:T])
                    v.tensor_copy(typ_f[:], typ_i[:]).then_inc(s_float, 1)
                    v.tensor_copy(rel_f[:], rel_i[:])
                    dve.wait_ge(s_masks, n_masks)
                    step.link(v.tensor_tensor(prod1[:], bcast(w1_rep[:].unsqueeze(1), [P, 2, HID]), a1_rep[:],
                                              ALU.mult))
                    step.link(v.tensor_reduce(score1[:].rearrange("p (k h) -> p k h", k=2),
                                              prod1[:].rearrange("p k (h c) -> p k h c", c=CH), AX_X, ALU.add))
                    v.tensor_tensor(bd_score[:], bcast(score1[:].unsqueeze(1), [P, 8, 2 * HEADS1]),
                                    bcast(mask8[:].unsqueeze(2), [P, 8, 2 * HEADS1]), ALU.mult)
                    v.tensor_tensor(bd_root1[:], bcast(root1_rep[:].unsqueeze(1), [P, 8, CH]),
                                    bcast(mask8[:].unsqueeze(2), [P, 8, CH]), ALU.mult)
                    v.tensor_tensor(bd_root2[:], bcast(root2_rep[:].unsqueeze(1), [P, 4, FEAT]),
                                    bcast(mask4[:].unsqueeze(2), [P, 4, FEAT]), ALU.mult)
                    for j in range(2):
                        v.tensor_tensor(w1_half[:, j], w1_rep[0:HID, :].rearrange("p (h c) -> p h c", c=CH),
                                        bcast(mask8[0:HID, 3 * j:3 * j + 3].unsqueeze(2), [HID, HEADS1, CH]), ALU.mult)
                    v.tensor_scalar(b1_col[:, 1:2], b1_col[:, 0:1], 1.0 / SELU_ALPHA, None, ALU.mult)
                    v.tensor_scalar(w2_ext[:, 0:CH], w2_raw[:], SELU_SCALE * SELU_ALPHA, None, ALU.mult)
                    step.link(v.tensor_scalar(wf_rep[:], wf_rep[:], SELU_SCALE * SELU_ALPHA, None, ALU.mult))
                    step.link(v.tensor_tensor(prod2[:], bcast(w2_ext[:, 0:CH].unsqueeze(1), [HID, 2, CH]), a2_rep[:],
                                              ALU.mult))
                    v.tensor_reduce(w2_ext[:, CH:CH + 2], prod2[:], AX_X, ALU.add)
                    v.tensor_tensor(bd_wf[:], bcast(wf_rep[:].unsqueeze(1), [P, 4, FEAT]),
                                    bcast(mask4[:].unsqueeze(2), [P, 4, FEAT]), ALU.mult)
                    for k in range(3):
                        last = v.tensor_scalar(wa_wide[:, k], ones[0:FEAT, :], wa_sb[:, k:k + 1], None, ALU.mult)
                    last.then_inc(s_wts, 1)
                    dve.wait_ge(s_prods, 1)
                    v.tensor_scalar(w2_const[:], ps[:, 1536:1536 + CH + 2], -1.0, None, ALU.mult)
                    v.tensor_tensor(wf_const[:], bf_row[:], ps[:, 1600:1600 + FEAT], ALU.subtract)
                    v.tensor_copy(c_row[:].rearrange("p k f -> p (k f)"), ps[:, 1664:1664 + 3 * FEAT])

                @block.tensor
                def _(pe):
                    pe.wait_ge(s_masks, n_masks)
                    pe.wait_ge(s_float, 1)
                    for n, rows_f in enumerate((src_f, dst_f, typ_f)):
                        for k in range(4):
                            col = 512 * n + P * k
                            last = nc.tensor.transpose(ps[0:QT, col:col + P], rows_f[:, QT * k:QT * (k + 1)], ident[:])
                        last.then_inc(s_rows_t, 1)
                    pe.wait_ge(s_wts, 1)
                    nc.tensor.matmul(ps[:, 1536:1536 + CH + 2], ones[0:HID, :], w2_ext[:], start=True, stop=True)
                    nc.tensor.matmul(ps[:, 1600:1600 + FEAT], ones[0:CH, :], wf_rep[0:CH, :], start=True, stop=True)
                    for k in range(3):
                        col = 1664 + FEAT * k
                        nc.tensor.matmul(ps[:, col:col + FEAT], wa_wide[:, k], ws_sb[:], start=True, stop=True)
                    nc.tensor.matmul(ps[0:RELS, 2048:2048 + FEAT * FEAT], comp_t[:],
                                     basis[:].rearrange("b i o -> b (i o)"), start=True, stop=True).then_inc(s_prods, 1)

                @block.scalar
                def _(act):
                    for n in range(3):
                        act.wait_ge(s_rows_t, n + 1)
                        nc.scalar.copy(rows[:, n], ps[0:QT, 512 * n:512 * (n + 1)].rearrange("q (k p) -> q k p", p=P)
                                       ).then_inc(s_rows, 1)
                    act.wait_ge(s_prods, 1)
                    nc.scalar.copy(w_flat[:], ps[0:RELS, 2048:2048 + FEAT * FEAT].rearrange("r (i o) -> r i o", o=FEAT)
                                   ).then_inc(s_flat, 1)

        def layer_norm_relu(dve, step, rows_in, rows_out, t, q, k):
            v = nc.vector
            step.link(v.tensor_reduce(t["sum"][:, 0:q], rows_in, AX_X, ALU.add))
            step.link(v.scalar_tensor_tensor(t["cent"][:, 0:q], bcast(t["sum"][:, 0:q].unsqueeze(2), [P, q, FEAT]),
                                             -1.0 / FEAT, rows_in, ALU.mult, ALU.add))
            step.link(v.tensor_tensor(t["sq"][:, 0:q], t["cent"][:, 0:q], t["cent"][:, 0:q], ALU.mult))
            step.link(v.tensor_reduce(t["var"][:, 0:q], t["sq"][:, 0:q], AX_X, ALU.add))
            v.tensor_scalar(t["var"][:, 0:q], t["var"][:, 0:q], 1.0 / FEAT, EPS, ALU.mult, ALU.add
                            ).then_inc(t["var_ok"], 1)
            hold(dve, t["root_ok"], k + 1)
            step.link(v.reciprocal(t["var"][:, 0:q], t["root"][:, 0:q]))
            return v.scalar_tensor_tensor(rows_out, t["cent"][:, 0:q], 0.0,
                                          bcast(t["var"][:, 0:q].unsqueeze(2), [P, q, FEAT]), ALU.max, ALU.mult)

        LN_LINKS = 5

        def take_root(act, t, k):
            hold(act, t["var_ok"], k + 1)
            nc.scalar.activation(t["root"][:], t["var"][:], ACT.Sqrt).then_inc(t["root_ok"], 1)

        def ln_buffers(ctx, q, tag):
            return {"sum": sb(f"{tag}_ln_sum", [P, q], F32, ctx), "cent": sb(f"{tag}_ln_cent", [P, q, FEAT], F32, ctx),
                    "sq": sb(f"{tag}_ln_sq", [P, q, FEAT], F32, ctx), "var": sb(f"{tag}_ln_var", [P, q], F32, ctx),
                    "root": sb(f"{tag}_ln_root", [P, q], F32, ctx),
                    "var_ok": semaphore(ctx, f"{tag}_var_ok"),
                    "root_ok": semaphore(ctx, f"{tag}_root_ok")}

        counts_ctx = ExitStack()
        counts = sb("counts", [P, C, NREL], F32, counts_ctx)
        as2 = sb("as2", [P, C, 1], F32, counts_ctx)
        ad2 = sb("ad2", [P, C, 1], F32, counts_ctx)
        self2 = sb("self2", [P, C, 1], F32, counts_ctx)
        gat = ExitStack()
        as1 = sb("as1", [P, C, HEADS1], F32, gat)
        ad1 = sb("ad1", [P, C, HEADS1], F32, gat)
        self1 = sb("self1", [P, C, HEADS1], F32, gat)

        with ExitStack() as ctx:
            def sem(name):
                return semaphore(ctx, name)

            Q = 40
            HALF = C // Q // 2
            t = ln_buffers(ctx, Q, "d0")
            zero = sb("zero", [P, C // 20 * WIDTH1], F32, ctx)
            row = sb("row", [P, 2, Q, FEAT + HEADS1], F32, ctx)
            h_c = sb("h_c", [P, 2, Q * FEAT], F32, ctx)
            h_t = sb("h_t", [P, 2, Q * FEAT], F32, ctx)
            ps = psum_all(ctx, "ps_h0")
            z_ready, z_done = sem("z_ready"), sem("z_done")
            step_s = sem("step_s")
            norm_done, flip_done, copy_done, prod_done, out_done = (sem(n) for n in (
                "norm_done", "flip_done", "copy_done", "prod_done", "out_done"))
            store = [sem("store0"), sem("store1")]
            stored, m_done = sem("stored"), sem("m_done")
            NG = Q * FEAT // P
            tables = [*acc1, *acc2, *acc3, *acc4, *acc5, *acc6]
            with nc.Block() as block:
                @block.vector
                def _(dve):
                    v = nc.vector
                    v.memset(zero[:], 0.0).then_inc(z_ready, 1)
                    with dve.Fori(0, HALF) as i:
                        step = Steps(dve, step_s, i * 2 * (LN_LINKS + 1))
                        for b in range(2):
                            k = i * 2 + b
                            hold(dve, stored, k + 1)
                            hold(dve, copy_done, k + 1)
                            step.link(layer_norm_relu(dve, step, X[:, bass.ds(k * Q, Q), :],
                                                      h_c[:, b].rearrange("p (q f) -> p q f", f=FEAT), t, Q, k))
                            v.tensor_copy(row[:, b, :, 0:FEAT], h_c[:, b].rearrange("p (q f) -> p q f", f=FEAT)
                                          ).then_inc(norm_done, 1)

                @block.tensor
                def _(pe):
                    pe.sem_inc(flip_done, 2)
                    with pe.Fori(0, HALF) as i:
                        for b in range(2):
                            k = i * 2 + b
                            hold(pe, norm_done, k + 1)
                            hold(pe, copy_done, k + 1)
                            for g in range(NG):
                                last = nc.tensor.transpose(ps[:, 1024 * b + P * g:1024 * b + P * (g + 1)],
                                                           h_c[:, b, P * g:P * (g + 1)], ident[:])
                            last.then_inc(flip_done, 1)
                            hold(pe, copy_done, k + 3)
                            hold(pe, out_done, k + 1)
                            for g in range(NG):
                                col = 2048 + 512 * b + 48 * g
                                last = nc.tensor.matmul(ps[:, col:col + 48], h_t[:, b, P * g:P * (g + 1)],
                                                        bd_score[:].rearrange("p j s -> p (j s)"), start=True, stop=True)
                            last.then_inc(prod_done, 1)

                @block.scalar
                def _(act):
                    act.wait_ge(z_ready, 1)
                    for table in tables:
                        piece = C * table.shape[1] // 20
                        act.dma_start(flat(table).rearrange("p (a z) -> p a z", z=piece),
                                      bcast(zero[:, 0:piece].unsqueeze(1), [P, 20, piece])).then_inc(z_done, 16)
                    act.sem_inc(copy_done, 2)
                    act.sem_inc(out_done, 2)
                    with act.Fori(0, HALF) as i:
                        for b in range(2):
                            k = i * 2 + b
                            take_root(act, t, k)
                            hold(act, flip_done, k + 3)
                            nc.scalar.copy(h_t[:, b], ps[:, 1024 * b:1024 * b + Q * FEAT]).then_inc(copy_done, 1)
                            hold(act, prod_done, k + 1)
                            view = ps[:, 2048 + 512 * b:2048 + 512 * b + 6 * Q].rearrange("p (q s) -> p q s", s=6)
                            nc.scalar.copy(row[:, b, :, FEAT:FEAT + HEADS1], view[:, :, 0:HEADS1])
                            nc.scalar.copy(as1[:, bass.ds(k * Q, Q), :], view[:, :, 0:HEADS1])
                            nc.scalar.copy(ad1[:, bass.ds(k * Q, Q), :], view[:, :, HEADS1:2 * HEADS1]
                                           ).then_inc(out_done, 1)

                @block.gpsimd
                def _(pool):
                    pool.sem_inc(stored, 2)
                    with pool.Fori(0, HALF) as i:
                        for b in range(2):
                            k = i * 2 + b
                            hold(pool, out_done, k + 3)
                            hold(pool, norm_done, k + 1)
                            pool.dma_start(by_node(t_gat1)[:, bass.ds(k * Q, Q), :], row[:, b]).then_inc(store[b], 16)
                            hold(pool, store[b], i * 16 + 16)
                            pool.sem_inc(stored, 1)

                @block.sync
                def _(sp):
                    sp.wait_ge(out_done, 2 * HALF + 2)
                    for table in max1:
                        sp.dma_start(by_node(table), as1[:]).then_inc(m_done, 16)
                    sp.wait_ge(m_done, 16 * B)
                    sp.wait_ge(z_done, 16 * len(tables))

        def segment_max(tag, table, replicas, H, F, keep, first):
            W = F + H
            with ExitStack() as ctx:
                def tmp(name, shape, dt=F32):
                    return sb(f"{tag}_{name}", shape, dt, ctx)

                def sem(name):
                    return semaphore(ctx, f"{tag}_{name}")

                rowd = tmp("rowd", [P, 2, B, P])
                rows_ = tmp("rows", [P, 2, B, P]) if first else None
                ring = tmp("ring", [P, 2, B, W])
                cur = tmp("cur", [P, 2, B, H])
                new = tmp("new", [P, 2, B, H])
                st_g, st_d, st_u = (tmp(n, [P, 2, B], I32) for n in ("st_g", "st_d", "st_u"))
                own = tmp("own", [P, 2, B])
                pen = tmp("pen", [P, B, P])
                lone = tmp("lone", [P, B, P])
                reps = tmp("reps", [P, 2, B])
                part = tmp("part", [P, 2, B])
                masked = tmp("masked", [P, B, H, P])
                group = tmp("group", [P, B, H])
                ps = psum_all(ctx, f"{tag}_ps")
                pv = ps[:, 0:B * 512].rearrange("p (s z) -> p s z", z=512)
                rows_in = [sem("rows_in0"), sem("rows_in1")]
                rows_free = sem("rows_free")
                gat_in = [sem("gat_in0"), sem("gat_in1")]
                cur_in = [sem("cur_in0"), sem("cur_in1")]
                kept = sem("kept")
                masked_ok = sem("masked_ok")
                flipped = sem("flipped")
                new_ok = sem("new_ok")
                staged = sem("staged")
                scattered = sem("scattered")
                step_s = sem("step")
                ND = 2 if first else 1
                with nc.Block() as block:
                    @block.sync
                    def _(sp):
                        with sp.Fori(0, ITER) as i:
                            for b in range(2):
                                k = i * 2 + b
                                hold(sp, rows_free, k + 1)
                                sp.dma_start(rowd[:, b].rearrange("p s j -> p (s j)"),
                                             row_dst.rearrange("(k s) j -> k (s j)", s=B)[k].partition_broadcast(P)
                                             ).then_inc(rows_in[b], 16)
                                if first:
                                    sp.dma_start(rows_[:, b].rearrange("p s j -> p (s j)"),
                                                 row_src.rearrange("(k s) j -> k (s j)", s=B)[k].partition_broadcast(P)
                                                 ).then_inc(rows_in[b], 16)

                    @block.gpsimd
                    def _(pool):
                        g = nc.gpsimd

                        def gather(b, slots):
                            for s in slots:
                                pool.indirect_dma_start(ring[:, b, s, :], None, table,
                                                        bass.IndirectOffsetOnAxis(st_g[:, b, s:s + 1], 0)
                                                        ).then_inc(gat_in[b], 16)

                        pool.dma_start(primer, primed[:]).then_inc(scattered, 16)
                        for b in range(2):
                            g.tensor_copy(st_g[:, b], src_i[:, B * b:B * (b + 1)]).then_inc(staged, 1)
                        pool.wait_ge(staged, 2)
                        for b in range(2):
                            gather(b, range(B))
                        with pool.Fori(0, ITER) as i:
                            for b in range(2):
                                k = i * 2 + b
                                base = i * 6 + 3 * b + 2
                                hold(pool, scattered, (k * B + 1) * 16)
                                g.tensor_copy(st_d[:, b], dst_i[:, bass.ds(k * B, B)]).then_inc(staged, 1)
                                hold(pool, staged, base + 1)
                                for s in range(B):
                                    pool.indirect_dma_start(cur[:, b, s, :], None, replicas[s],
                                                            bass.IndirectOffsetOnAxis(st_d[:, b, s:s + 1], 0)
                                                            ).then_inc(cur_in[b], 16)
                                hold(pool, kept, k + 1)
                                hold(pool, masked_ok, k + 1)
                                g.tensor_copy(st_g[:, b], src_i[:, bass.ds(k * B + 2 * B, B)]).then_inc(staged, 1)
                                hold(pool, staged, base + 2)
                                gather(b, range(4))
                                hold(pool, new_ok, k + 1)
                                g.tensor_copy(st_u[:, b], uniq_dst[:, bass.ds(k * B, B)]).then_inc(staged, 1)
                                hold(pool, staged, base + 3)
                                for s in range(B):
                                    pool.indirect_dma_start(replicas[s],
                                                            bass.IndirectOffsetOnAxis(st_u[:, b, s:s + 1], 0),
                                                            new[:, b, s, :], None).then_inc(scattered, 16)
                                gather(b, range(4, B))
                        pool.wait_ge(scattered, (2 * ITER * B + 1) * 16)
                        for b in range(2):
                            pool.wait_ge(gat_in[b], (ITER + 1) * B * 16)

                    @block.scalar
                    def _(act):
                        with act.Fori(0, ITER) as i:
                            for b in range(2):
                                hold(act, gat_in[b], i * (B * 16) + B * 16)
                                nc.scalar.copy(keep[:, bass.ds((i * 2 + b) * B, B), :], ring[:, b]).then_inc(kept, 1)

                    @block.vector
                    def _(dve):
                        v = nc.vector
                        dve.sem_inc(rows_free, 2)
                        links = (2 + 2 + 3 if first else 2) + 1
                        with dve.Fori(0, ITER) as i:
                            step = Steps(dve, step_s, i * 2 * links)
                            for b in range(2):
                                k = i * 2 + b
                                cols = bass.ds(k * B, B)
                                v.tensor_copy(own[:, 1], src_f[:, cols])
                                step.link(v.tensor_copy(own[:, 0], dst_f[:, cols]))
                                hold(dve, rows_in[b], i * (16 * ND) + 16 * ND)
                                for s in range(B):
                                    last = v.tensor_scalar(pen[:, s], rowd[:, b, s], own[:, 0, s:s + 1], FAR,
                                                           ALU.not_equal, ALU.mult)
                                if first:
                                    step.link(last)
                                    for n, rr in enumerate((rowd, rows_)):
                                        for s in range(B):
                                            last = v.scalar_tensor_tensor(lone[:, s], rr[:, b, s], own[:, n, s:s + 1],
                                                                          earlier[:], ALU.is_equal, ALU.mult,
                                                                          accum_out=reps[:, n, s:s + 1])
                                        step.link(last)
                                    step.link(v.tensor_scalar(part[:], own[:], -1.0, spare[:], ALU.mult, ALU.add))
                                    step.link(v.scalar_tensor_tensor(part[:], reps[:], 0.0, part[:], ALU.is_gt, ALU.mult))
                                    v.tensor_tensor(uniq_dst[:, cols], part[:, 0], own[:, 0], ALU.add)
                                    step.link(v.tensor_tensor(uniq_src[:, cols], part[:, 1], own[:, 1], ALU.add))
                                else:
                                    step.link(last)
                                dve.sem_inc(rows_free, 1)
                                hold(dve, gat_in[b], i * (B * 16) + B * 16)
                                v.tensor_tensor(masked[:], bcast(pen[:].unsqueeze(2), [P, B, H, P]),
                                                bcast(ring[:, b, :, F:W].unsqueeze(3), [P, B, H, P]),
                                                ALU.add).then_inc(masked_ok, 1)
                                hold(dve, flipped, k + 1)
                                step.link(v.tensor_reduce(
                                    group[:], pv[:, :, 0:H * P].rearrange("p s (h j) -> p s h j", j=P), AX_X, ALU.max))
                                hold(dve, cur_in[b], i * (B * 16) + B * 16)
                                v.tensor_tensor(new[:, b], group[:], cur[:, b], ALU.max).then_inc(new_ok, 1)
                            assert step.n == 2 * links, step.n

                    @block.tensor
                    def _(pe):
                        with pe.Fori(0, ITER) as i:
                            for b in range(2):
                                hold(pe, masked_ok, i * 2 + b + 1)
                                for s in range(B):
                                    for h in range(H):
                                        last = nc.tensor.transpose(pv[:, s, h * P:(h + 1) * P], masked[:, s, h], ident[:])
                                last.then_inc(flipped, 1)

        def scatter_pass(tag, gathers, key, W, accs, messages, links, exp=None, expand=0, weights=None, extra=None):
            key_rows, key_f, key_u = key
            with ExitStack() as ctx:
                def tmp(name, shape, dt=F32):
                    return sb(f"{tag}_{name}", shape, dt, ctx)

                def sem(name):
                    return semaphore(ctx, f"{tag}_{name}")

                NG = len(gathers)
                NM = expand * P if expand else W
                keys = tmp("keys", [P, 2, B, P])
                same = tmp("same", [P, 2, B, P])
                own = tmp("own", [P, B])
                rings = [tmp(f"ring{n}", [P, 2, B, w]) for n, (_, _, w) in enumerate(gathers)]
                st_g = tmp("st_g", [P, 2, NG, B], I32)
                st_u = tmp("st_u", [P, 2, B], I32)
                msg = tmp("msg", [P, 2, B, NM])
                summed = tmp("summed", [P, expand, B, P]) if expand else None
                rows = tmp("rows", [P, 2, B, W])
                typs = tmp("typs", [P, 2, B, P]) if extra else None
                pick = tmp("pick", [P, B, P]) if extra else None
                ps = psum_all(ctx, f"{tag}_ps")
                ps_rows = [ps[:, 512 * b:512 * b + B * W].rearrange("p (s w) -> p s w", w=W) for b in range(2)]
                ps_mid = ps[:, 1024:1024 + 2048]
                keys_in = [sem("keys_in0"), sem("keys_in1")]
                gat_in = [sem("gat_in0"), sem("gat_in1")]
                same_ok = sem("same_ok")
                msg_ok = sem("msg_ok")
                pre_ok = sem("pre_ok")
                exp_ok = sem("exp_ok")
                pick_ok = sem("pick_ok")
                mats_ok = sem("mats_ok")
                sum_ok = sem("sum_ok")
                copy_ok = sem("copy_ok")
                prod_ok = sem("prod_ok")
                rows_ok = sem("rows_ok")
                rows_free = sem("rows_free")
                staged = sem("staged")
                scat = [sem("scat0"), sem("scat1")]
                step_s = sem("step")
                ND = 2 if extra else 1
                env = dict(rings=rings, msg=msg, pre_ok=pre_ok, exp_ok=exp_ok, pick_ok=pick_ok, mats_ok=mats_ok,
                           ps_mid=ps_mid, pick=pick, typs=typs)
                env["t"] = {}
                with nc.Block() as block:
                    @block.sync
                    def _(sp):
                        with sp.Fori(0, ITER) as i:
                            for b in range(2):
                                k = i * 2 + b
                                hold(sp, same_ok, k + 1)
                                sp.dma_start(keys[:, b].rearrange("p s j -> p (s j)"),
                                             key_rows.rearrange("(k s) j -> k (s j)", s=B)[k].partition_broadcast(P)
                                             ).then_inc(keys_in[b], 16)
                                if extra:
                                    hold(sp, pick_ok, k + 1)
                                    sp.dma_start(typs[:, b].rearrange("p s j -> p (s j)"),
                                                 row_typ.rearrange("(k s) j -> k (s j)", s=B)[k].partition_broadcast(P)
                                                 ).then_inc(keys_in[b], 16)

                    @block.gpsimd
                    def _(pool):
                        g = nc.gpsimd

                        def gather(b, s):
                            for n, (table, _, _) in enumerate(gathers):
                                pool.indirect_dma_start(rings[n][:, b, s, :], None, table,
                                                        bass.IndirectOffsetOnAxis(st_g[:, b, n, s:s + 1], 0)
                                                        ).then_inc(gat_in[b], 16)

                        pool.sem_inc(rows_free, 1)
                        for r in range(2):
                            pool.dma_start(primer, primed[:]).then_inc(scat[r], 16)
                            pool.wait_ge(scat[r], 16)
                        for b in range(2):
                            for n, (_, idx, _) in enumerate(gathers):
                                g.tensor_copy(st_g[:, b, n], idx[:, B * b:B * (b + 1)]).then_inc(staged, 1)
                        pool.wait_ge(staged, 2 * NG)
                        for b in range(2):
                            for s in range(B):
                                gather(b, s)
                        with pool.Fori(0, ITER) as i:
                            count = [0, 0]
                            for b in range(2):
                                k = i * 2 + b
                                hold(pool, msg_ok, k + 1)
                                hold(pool, rows_ok, k + 3)
                                for n, (_, idx, _) in enumerate(gathers):
                                    g.tensor_copy(st_g[:, b, n], idx[:, bass.ds(k * B + 2 * B, B)]).then_inc(staged, 1)
                                g.tensor_copy(st_u[:, b], key_u[:, bass.ds(k * B, B)]).then_inc(staged, 1)
                                hold(pool, staged, (i * 2 + b + 1) * (NG + 1) + 2 * NG)
                                for s in range(B):
                                    gather(b, s)
                                    r = (s + b) % 2
                                    hold(pool, scat[r], (i * B + count[r] + 1) * 16)
                                    pool.indirect_dma_start(accs[r], bass.IndirectOffsetOnAxis(st_u[:, b, s:s + 1], 0),
                                                            rows[:, b, s, :], None, compute_op=ALU.add
                                                            ).then_inc(scat[r], 16)
                                    count[r] += 1
                                    if s == 1:
                                        pool.sem_inc(rows_free, 1)
                        for r in range(2):
                            pool.wait_ge(scat[r], (ITER * B + 1) * 16)
                        for b in range(2):
                            pool.wait_ge(gat_in[b], (ITER + 1) * B * NG * 16)

                    @block.vector
                    def _(dve):
                        v = nc.vector
                        dve.sem_inc(same_ok, 2)
                        if extra:
                            dve.sem_inc(pick_ok, 2)
                        with dve.Fori(0, ITER) as i:
                            step = Steps(dve, step_s, i * (2 * (links + 1)))
                            for b in range(2):
                                k = i * 2 + b
                                step.link(v.tensor_copy(own[:], key_f[:, bass.ds(k * B, B)]))
                                hold(dve, keys_in[b], i * (16 * ND) + 16 * ND)
                                hold(dve, prod_ok, k + 1)
                                v.tensor_tensor(same[:, b], keys[:, b], bcast(own[:].unsqueeze(2), [P, B, P]),
                                                ALU.is_equal).then_inc(same_ok, 1)
                                gathered = (gat_in[b], i * (B * NG * 16) + B * NG * 16)
                                messages(dve, step, env, k, b, gathered).then_inc(msg_ok, 1)
                            assert step.n == 2 * (links + 1), step.n

                    @block.tensor
                    def _(pe):
                        mm = nc.tensor.matmul
                        pe.sem_inc(prod_ok, 2)
                        with pe.Fori(0, ITER) as i:
                            for b in range(2):
                                k = i * 2 + b
                                if extra:
                                    hold(pe, pick_ok, k + 3)
                                    for s in range(B):
                                        last = mm(ps_mid[:, 256 * s:256 * (s + 1)], pick[:, s],
                                                  w_rel[:].rearrange("p i o -> p (i o)"), start=True, stop=True)
                                    last.then_inc(mats_ok, 1)
                                hold(pe, msg_ok, k + 1)
                                if expand:
                                    hold(pe, copy_ok, k + 1)
                                    for a in range(expand):
                                        for s in range(B):
                                            last = mm(ps_mid[:, 1024 * a + P * s:1024 * a + P * (s + 1)],
                                                      msg[:, b, s, P * a:P * (a + 1)], same[:, b, s],
                                                      start=True, stop=True)
                                    last.then_inc(sum_ok, 1)
                                    hold(pe, copy_ok, k + 2)
                                hold(pe, rows_ok, k + 1)
                                for s in range(B):
                                    if expand:
                                        for a in range(expand):
                                            last = mm(ps_rows[b][:, s], summed[:, a, s], weights(a),
                                                      start=(a == 0), stop=(a == expand - 1))
                                    else:
                                        last = mm(ps_rows[b][:, s], same[:, b, s], msg[:, b, s], start=True, stop=True)
                                last.then_inc(prod_ok, 1)

                    @block.scalar
                    def _(act):
                        act.sem_inc(rows_ok, 2)
                        if expand:
                            act.sem_inc(copy_ok, 1)
                        with act.Fori(0, ITER) as i:
                            for b in range(2):
                                k = i * 2 + b
                                if exp:
                                    hold(act, pre_ok, k + 1)
                                    exp(env, b).then_inc(exp_ok, 1)
                                if expand:
                                    hold(act, sum_ok, k + 1)
                                    for a in range(expand):
                                        last = nc.scalar.copy(summed[:, a].rearrange("p s j -> p (s j)"),
                                                              ps_mid[:, 1024 * a:1024 * a + B * P])
                                    last.then_inc(copy_ok, 1)
                                hold(act, prod_ok, k + 3)
                                hold(act, rows_free, k + 1)
                                nc.scalar.copy(rows[:, b], ps_rows[b]).then_inc(rows_ok, 1)

        key_dst = (row_dst, dst_f, uniq_dst)
        key_src = (row_src, src_f, uniq_src)

        kept1 = ExitStack()
        keep1 = sb("keep1", [P, T, FEAT + HEADS1], F32, kept1)
        segment_max("m1", t_gat1, max1, HEADS1, FEAT, keep1, True)

        def settle_max(tag, replicas, H, as_, ad_, self_, table, counts):
            PIECES = 2
            CP = C // PIECES
            with ExitStack() as ctx:
                def sem(name):
                    return semaphore(ctx, f"{tag}_{name}")

                W = 2 * H + (NREL if counts is not None else 0)
                two = sb(f"{tag}_two", [P, 2, C, H], F32, ctx)
                m = sb(f"{tag}_m", [P, C, H], F32, ctx)
                e = self_
                row = sb(f"{tag}_row", [P, CP, W], F32, ctx)
                in_ = [sem("in0"), sem("in1")]
                step_s, row_ok, arg_ok, out_s = sem("step"), sem("row_ok"), sem("arg_ok"), sem("out")
                with nc.Block() as block:
                    @block.sync
                    def _(sp):
                        for n, rep in enumerate(replicas):
                            if n >= 2:
                                sp.wait_ge(step_s, n - 1)
                            sp.dma_start(two[:, n % 2], by_node(rep)).then_inc(in_[n % 2], 16)
                        for piece in range(PIECES):
                            sp.wait_ge(row_ok, piece + 1)
                            sp.dma_start(by_node(table)[:, piece * CP:(piece + 1) * CP, :], row[:]
                                         ).then_inc(out_s, 16)
                        sp.wait_ge(out_s, 16 * PIECES)

                    @block.vector
                    def _(dve):
                        v = nc.vector
                        step = Steps(dve, step_s)
                        for n in range(B):
                            dve.wait_ge(in_[n % 2], 16 * (n // 2 + 1))
                            step.link(v.tensor_copy(m[:], two[:, 0]) if n == 0 else
                                      v.tensor_tensor(m[:], m[:], two[:, n % 2], ALU.max))
                        step.link(v.tensor_tensor(m[:], m[:], ad_[:], ALU.add))
                        step.link(v.scalar_tensor_tensor(m[:], m[:], SLOPE, m[:], ALU.mult, ALU.max))
                        for piece in range(PIECES):
                            cols = slice(piece * CP, (piece + 1) * CP)
                            if piece:
                                dve.wait_ge(out_s, 16 * piece)
                            v.tensor_copy(row[:, :, 0:H], m[:, cols, :])
                            if counts is not None:
                                v.tensor_copy(row[:, :, 2 * H:W], counts[:, cols, :])
                            v.tensor_copy(row[:, :, H:2 * H], ad_[:, cols, :]).then_inc(row_ok, 1)
                        step.link(v.tensor_tensor(e[:], as_[:], ad_[:], ALU.add))
                        step.link(v.scalar_tensor_tensor(e[:], e[:], SLOPE, e[:], ALU.mult, ALU.max))
                        v.tensor_tensor(e[:], e[:], m[:], ALU.subtract).then_inc(arg_ok, 1)

                    @block.scalar
                    def _(act):
                        act.wait_ge(arg_ok, 1)
                        nc.scalar.activation(self_[:], e[:], ACT.Exp)

        settle_max("s1", max1, HEADS1, as1, ad1, self1, t_norm1, None)

        with ExitStack() as ctx:
            arg = sb("arg1", [P, B, HEADS1], F32, ctx)
            wgt = sb("wgt1", [P, B, HEADS1], F32, ctx)
            rel = sb("rel1", [P, B], F32, ctx)

            def gat1_messages(dve, step, env, k, b, gathered):
                v = nc.vector
                cols = bass.ds(k * B, B)
                norm, msg = env["rings"][0], env["msg"]
                hold(dve, *gathered)
                v.tensor_copy(rel[:], rel_f[:, cols])
                step.link(v.tensor_tensor(arg[:], keep1[:, cols, FEAT:FEAT + HEADS1], norm[:, b, :, HEADS1:2 * HEADS1],
                                          ALU.add))
                step.link(v.scalar_tensor_tensor(arg[:], arg[:], SLOPE, arg[:], ALU.mult, ALU.max))
                v.tensor_tensor(arg[:], arg[:], norm[:, b, :, 0:HEADS1], ALU.subtract).then_inc(env["pre_ok"], 1)
                v.tensor_tensor(msg[:, b, :, WIDTH1 - NREL:WIDTH1], bcast(rel[:].unsqueeze(2), [P, B, NREL]),
                                bcast(iota8[:].unsqueeze(1), [P, B, NREL]), ALU.is_equal)
                hold(dve, env["exp_ok"], k + 1)
                v.tensor_copy(msg[:, b, :, HEADS1 * FEAT:HEADS1 * FEAT + HEADS1], wgt[:])
                return v.tensor_tensor(
                    msg[:, b, :, 0:HEADS1 * FEAT].rearrange("p s (h f) -> p s h f", f=FEAT),
                    bcast(keep1[:, cols, 0:FEAT].unsqueeze(2), [P, B, HEADS1, FEAT]),
                    bcast(wgt[:].unsqueeze(3), [P, B, HEADS1, FEAT]), ALU.mult)

            scatter_pass("g1", [(t_norm1, dst_i, 2 * HEADS1)], key_dst, WIDTH1, acc1, gat1_messages, 2,
                         exp=lambda env, b: nc.scalar.activation(wgt[:], arg[:], ACT.Exp))
        kept1.close()

        def stream(sp, half, Q, loads, in_, table, row, row_ok, out_s, stored):
            def load(k, b):
                for to, frm in loads:
                    sp.dma_start(to[:, b], by_node(frm)[:, bass.ds(k * Q, Q), :]).then_inc(in_[b], 16)

            def put(k, b):
                hold(sp, row_ok, k + 3)
                if table is None:
                    return
                sp.dma_start(by_node(table)[:, bass.ds(k * Q, Q), :], row[:, b]).then_inc(out_s[b], 16)

            sp.sem_inc(stored, 2)
            load(0, 0)
            load(1, 1)
            with sp.Fori(0, half - 1) as i:
                for b in range(2):
                    k = i * 2 + b
                    put(k, b)
                    load(k + 2, b)
                    if table is not None:
                        hold(sp, out_s[b], i * 16 + 16)
                    sp.sem_inc(stored, 1)
            for b in range(2):
                put(2 * (half - 1) + b, b)
            for b in range(2):
                if table is not None:
                    sp.wait_ge(out_s[b], 16 * half)
                sp.sem_inc(stored, 1)

        with ExitStack() as ctx:
            def tmp(name, shape, dt=F32):
                return sb(f"d2_{name}", shape, dt, ctx)

            def sem(name):
                return semaphore(ctx, f"d2_{name}")

            Q = 16
            PAIRS = Q // 2
            HALF = C // Q // 2
            HF = HEADS1 * FEAT
            a0, a1 = tmp("a0", [P, 2, Q, WIDTH1]), tmp("a1", [P, 2, Q, WIDTH1])
            hs = tmp("hs", [P, 2, Q, FEAT + HEADS1])
            agg = tmp("agg", [P, Q, WIDTH1])
            mix = tmp("mix", [P, 2, Q, HF])
            z = tmp("z", [P, Q, HEADS1])
            mix_t = tmp("mix_t", [HID, PAIRS * P])
            pos = tmp("pos", [HID, 4, 512])
            ex = tmp("ex", [HID, 4, 512])
            act_t = tmp("act_t", [HID, 4, 512])
            row = tmp("row", [P, 2, Q, CH + 1])
            ps = psum_all(ctx, "d2_ps")
            ps_o = ps[:, 3072:4096].rearrange("p (a z) -> p a z", z=512)[:, :, 0:8 * (CH + 2)].rearrange(
                "p a (n w) -> p a n w", w=CH + 2)
            in_ = [sem("in0"), sem("in1")]
            out_s = [sem("out0"), sem("out1")]
            step_s, pstep_s = sem("step"), sem("pstep")
            z_ok, rz_ok = sem("z_ok"), sem("rz_ok")
            mix_ok = sem("mix_ok")
            flip_ok, up_ok, down_ok = sem("flip_ok"), sem("up_ok"), sem("down_ok")
            copy_ok, exp_ok = sem("copy_ok"), sem("exp_ok")
            act_ok, row_ok = sem("act_ok"), sem("row_ok")
            stored, m_s = sem("stored"), sem("m_s")
            with nc.Block() as block:
                @block.sync
                def _(sp):
                    stream(sp, HALF, Q, [(a0, acc1[0]), (a1, acc1[1]), (hs, t_gat1)], in_,
                           t_gat2, row, row_ok, out_s, stored)
                    for table in max2:
                        sp.dma_start(by_node(table), as2[:]).then_inc(m_s, 16)
                    sp.wait_ge(m_s, 16 * B)

                @block.gpsimd
                def _(pool):
                    g = nc.gpsimd
                    pool.sem_inc(mix_ok, 2)
                    with pool.Fori(0, HALF) as i:
                        step = Steps(pool, pstep_s, i * 10, apart=True)
                        for b in range(2):
                            k = i * 2 + b
                            cols = bass.ds(k * Q, Q)
                            heads = mix[:, b].rearrange("p q (h f) -> p q h f", f=FEAT)
                            hold(pool, in_[b], i * 48 + 48)
                            hold(pool, flip_ok, k + 1)
                            step.link(g.tensor_tensor(agg[:], a0[:, b], a1[:, b], ALU.add))
                            step.link(g.tensor_tensor(z[:], agg[:, :, HF:HF + HEADS1], self1[:, cols, :], ALU.add))
                            pool.sem_inc(z_ok, 1)
                            step.link(g.tensor_copy(counts[:, cols, :], agg[:, :, WIDTH1 - NREL:WIDTH1]))
                            step.link(g.tensor_tensor(
                                heads, bcast(hs[:, b, :, 0:FEAT].unsqueeze(2), [P, Q, HEADS1, FEAT]),
                                bcast(self1[:, cols, :].unsqueeze(3), [P, Q, HEADS1, FEAT]), ALU.mult))
                            step.link(g.tensor_tensor(mix[:, b], mix[:, b], agg[:, :, 0:HF], ALU.add))
                            hold(pool, rz_ok, k + 1)
                            g.tensor_tensor(heads, heads, bcast(z[:].unsqueeze(3), [P, Q, HEADS1, FEAT]), ALU.mult
                                            ).then_inc(mix_ok, 1)

                @block.tensor
                def _(pe):
                    mm = nc.tensor.matmul
                    pe.sem_inc(flip_ok, 2)
                    with pe.Fori(0, HALF) as i:
                        for b in range(2):
                            k = i * 2 + b
                            hold(pe, mix_ok, k + 3)
                            for n in range(PAIRS):
                                last = nc.tensor.transpose(ps[0:HID, P * n:P * (n + 1)],
                                                           mix[:, b, 2 * n:2 * n + 2, :].rearrange("p a f -> p (a f)"),
                                                           ident[:])
                            last.then_inc(flip_ok, 1)
                            hold(pe, copy_ok, k + 1)
                            hold(pe, exp_ok, k * 4 + 4)
                            for u in range(4):
                                j, q = u // 2, u % 2
                                mm(ps[0:HID, 1024 + 512 * u:1536 + 512 * u],
                                   w1_half[:, j].rearrange("p h c -> p (h c)"), mix_t[:, 512 * q:512 * (q + 1)],
                                   start=True, stop=True).then_inc(up_ok, 1)
                            hold(pe, row_ok, k + 2)
                            for u in range(4):
                                j, q = u // 2, u % 2
                                hold(pe, act_ok, k * 4 + u + 1)
                                for n in range(4):
                                    node = 2 * (4 * q + n) + j
                                    last = mm(ps_o[:, node // 8, node % 8], act_t[:, u, P * n:P * (n + 1)], w2_ext[:],
                                              start=True, stop=True)
                            last.then_inc(down_ok, 1)

                @block.scalar
                def _(act):
                    act.sem_inc(exp_ok, 4)
                    with act.Fori(0, HALF) as i:
                        for b in range(2):
                            k = i * 2 + b
                            hold(act, flip_ok, k + 3)
                            nc.scalar.copy(mix_t[:], ps[0:HID, 0:PAIRS * P]).then_inc(copy_ok, 1)
                            for u in range(4):
                                hold(act, up_ok, k * 4 + u + 1)
                                view = ps[0:HID, 1024 + 512 * u:1536 + 512 * u]
                                nc.scalar.activation(pos[:, u], view, ACT.Relu, bias=b1_col[:, 1:2],
                                                     scale=1.0 / SELU_ALPHA)
                                nc.scalar.activation(ex[:, u], view, ACT.Exp, bias=b1_col[:, 0:1]).then_inc(exp_ok, 1)

                @block.vector
                def _(dve):
                    v = nc.vector
                    dve.sem_inc(row_ok, 2)
                    with dve.Fori(0, HALF) as i:
                        step = Steps(dve, step_s, i * 2)
                        for b in range(2):
                            k = i * 2 + b
                            hold(dve, z_ok, k + 1)
                            step.link(v.tensor_scalar(z[:], z[:], 1e-16, None, ALU.add))
                            v.reciprocal(z[:], z[:]).then_inc(rz_ok, 1)
                            for u in range(4):
                                hold(dve, exp_ok, k * 4 + u + 5)
                                v.scalar_tensor_tensor(act_t[:, u], ex[:, u], 1.0, pos[:, u], ALU.min, ALU.add
                                                       ).then_inc(act_ok, 1)
                            hold(dve, down_ok, k + 1)
                            hold(dve, stored, k + 1)
                            half = lambda ap: ap.rearrange("p (a n) w -> p a n w", n=8)
                            const = bcast(w2_const[:].unsqueeze(1).unsqueeze(1), [P, 2, 8, CH + 2])
                            for to, lo, hi in ((as2[:, bass.ds(k * Q, Q), :], CH, CH + 1),
                                               (ad2[:, bass.ds(k * Q, Q), :], CH + 1, CH + 2),
                                               (row[:, b], 0, CH + 1)):
                                last = v.tensor_tensor(half(to), ps_o[:, :, :, lo:hi], const[:, :, :, lo:hi], ALU.add)
                            last.then_inc(row_ok, 1)
        gat.close()

        kept2 = ExitStack()
        keep2 = sb("keep2", [P, T, CH + 1], F32, kept2)
        segment_max("m2", t_gat2, max2, 1, CH, keep2, False)
        settle_max("s2", max2, 1, as2, ad2, self2, t_norm2, counts)

        with ExitStack() as ctx:
            arg = sb("arg2", [P, B, 1], F32, ctx)
            wgt = sb("wgt2", [P, B, 1], F32, ctx)
            rel = sb("rel2", [P, B], F32, ctx)
            hot = sb("hot2", [P, B, NREL], F32, ctx)
            cnt = sb("cnt2", [P, B], F32, ctx)

            def gat2_messages(dve, step, env, k, b, gathered):
                v = nc.vector
                cols = bass.ds(k * B, B)
                norm, msg = env["rings"][0], env["msg"]
                hold(dve, *gathered)
                step.link(v.tensor_copy(rel[:], rel_f[:, cols]))
                step.link(v.tensor_tensor(arg[:], keep2[:, cols, CH:CH + 1], norm[:, b, :, 1:2], ALU.add))
                step.link(v.scalar_tensor_tensor(arg[:], arg[:], SLOPE, arg[:], ALU.mult, ALU.max))
                v.tensor_tensor(arg[:], arg[:], norm[:, b, :, 0:1], ALU.subtract).then_inc(env["pre_ok"], 1)
                step.link(v.tensor_tensor(hot[:], bcast(rel[:].unsqueeze(2), [P, B, NREL]),
                                          bcast(iota8[:].unsqueeze(1), [P, B, NREL]), ALU.is_equal))
                step.link(v.tensor_tensor(hot[:], hot[:], norm[:, b, :, 2:2 + NREL], ALU.mult))
                step.link(v.tensor_reduce(cnt[:], hot[:], AX_X, ALU.add))
                step.link(v.tensor_scalar(cnt[:], cnt[:], 1.0, None, ALU.max))
                v.reciprocal(inv_cnt[:, cols], cnt[:])
                hold(dve, env["exp_ok"], k + 1)
                v.tensor_copy(msg[:, b, :, CH:CH + 1], wgt[:])
                return v.tensor_tensor(msg[:, b, :, 0:CH], keep2[:, cols, 0:CH], bcast(wgt[:], [P, B, CH]), ALU.mult)

            scatter_pass("g2", [(t_norm2, dst_i, 2 + NREL)], key_dst, WIDTH2, acc2, gat2_messages, 7,
                         exp=lambda env, b: nc.scalar.activation(wgt[:], arg[:], ACT.Exp))
        kept2.close()

        QN = 40
        HN = C // QN // 2

        def node_pass(tag, loads, table, width_out, prepare, nodes, links, flips=None, wide=0, bd=None, act_mid=None, prep_links=1, norm=True):
            with ExitStack() as ctx:
                def tmp(name, shape, dt=F32):
                    return sb(f"{tag}_{name}", shape, dt, ctx)

                def sem(name):
                    return semaphore(ctx, f"{tag}_{name}")

                ins = [(tmp(f"in{n}", [P, 2, QN, t.shape[1]]), t) for n, t in enumerate(loads)]
                row = tmp("row", [P, 2, QN, width_out])
                t = ln_buffers(ctx, QN, tag) if norm else None
                ps = psum_all(ctx, f"{tag}_ps")
                in_ = [sem("in0"), sem("in1")]
                out_s = [sem("out0"), sem("out1")]
                names = ("step", "pstep", "prep_ok", "mid_ok", "exp_ok", "flip_in", "flip_ok", "copy_ok",
                         "prod_ok", "used_ok", "row_ok", "stored")
                env = {n: sem(n) for n in names}
                env.update(ins=[a for a, _ in ins], row=row, t=t, tmp=tmp, ps_out=ps[:, 2048:2048 + QN * max(width_mid(
                    wide, flips), 1)] if flips else None)
                w_in = flips or 0
                cols_in = QN * w_in
                n_flip = cols_in // P
                flipped = tmp("flipped", [P, cols_in]) if flips else None
                env["flip_src"] = None
                extra = prepare("alloc", None, env, None, None, None) or {}
                env.update(extra)
                with nc.Block() as block:
                    @block.sync
                    def _(sp):
                        stream(sp, HN, QN, ins, in_, table, row, env["row_ok"], out_s, env["stored"])

                    @block.gpsimd
                    def _(pool):
                        with pool.Fori(0, HN) as i:
                            step = Steps(pool, env["pstep"], i * 2 * prep_links, apart=True)
                            for b in range(2):
                                k = i * 2 + b
                                hold(pool, in_[b], i * (16 * len(loads)) + 16 * len(loads))
                                hold(pool, env["used_ok"], k + 1)
                                prepare("run", pool, env, step, k, b)
                                pool.sem_inc(env["prep_ok"], 1)
                            assert step.n == 2 * prep_links, step.n

                    @block.vector
                    def _(dve):
                        dve.sem_inc(env["row_ok"], 2)
                        dve.sem_inc(env["used_ok"], 1)
                        with dve.Fori(0, HN) as i:
                            step = Steps(dve, env["step"], i * 2 * links)
                            for b in range(2):
                                k = i * 2 + b
                                hold(dve, env["prep_ok"], k + 1)
                                hold(dve, env["stored"], k + 1)
                                nodes(dve, env, step, k, b)
                            assert step.n == 2 * links, step.n

                    if flips:
                        @block.tensor
                        def _(pe):
                            with pe.Fori(0, HN) as i:
                                for b in range(2):
                                    k = i * 2 + b
                                    hold(pe, env["flip_in"], k + 1)
                                    for n in range(n_flip):
                                        last = nc.tensor.transpose(ps[:, P * n:P * (n + 1)],
                                                                   env["flip_src"](b)[:, P * n:P * (n + 1)], ident[:])
                                    last.then_inc(env["flip_ok"], 1)
                                    hold(pe, env["copy_ok"], k + 1)
                                    hold(pe, env["used_ok"], k + 1)
                                    for n in range(n_flip):
                                        last = nc.tensor.matmul(ps[:, 2048 + wide * n:2048 + wide * (n + 1)],
                                                                flipped[:, P * n:P * (n + 1)], bd, start=True, stop=True)
                                    last.then_inc(env["prod_ok"], 1)

                    if flips or norm:
                        @block.scalar
                        def _(act):
                            with act.Fori(0, HN) as i:
                                for b in range(2):
                                    k = i * 2 + b
                                    if act_mid:
                                        hold(act, env["mid_ok"], k + 1)
                                        act_mid(env, b).then_inc(env["exp_ok"], 1)
                                    if flips:
                                        hold(act, env["flip_ok"], k + 1)
                                        nc.scalar.copy(flipped[:], ps[:, 0:cols_in]).then_inc(env["copy_ok"], 1)
                                    if norm:
                                        take_root(act, t, k)

        def width_mid(wide, flips):
            return wide * (flips or 0) // P

        def columns(ap, w):
            return ap.rearrange("p (q w) -> p q w", w=w)

        def d4_prepare(what, pool, env, step, k, b):
            if what == "alloc":
                tmp = env["tmp"]
                new = dict(agg=tmp("agg", [P, QN, WIDTH2]), mix=tmp("mix", [P, QN, CH]), z=tmp("z", [P, QN, 1]),
                           pos=tmp("pos", [P, QN, CH]), ex=tmp("ex", [P, QN, CH]))
                new["flip_src"] = lambda b: new["ex"][:].rearrange("p q f -> p (q f)")
                return new
            g = nc.gpsimd
            a0, a1, hs = env["ins"]
            agg, mix, z = env["agg"], env["mix"], env["z"]
            cols = bass.ds(k * QN, QN)
            step.link(g.tensor_tensor(agg[:], a0[:, b], a1[:, b], ALU.add))
            step.link(g.tensor_tensor(z[:], agg[:, :, CH:CH + 1], self2[:, cols, :], ALU.add))
            step.link(g.tensor_tensor(mix[:], hs[:, b, :, 0:CH], bcast(self2[:, cols, :], [P, QN, CH]), ALU.mult))
            step.link(g.tensor_tensor(mix[:], mix[:], agg[:, :, 0:CH], ALU.add))

        def d4_nodes(dve, env, step, k, b):
            v = nc.vector
            mix, z, pos, ex, row = env["mix"], env["z"], env["pos"], env["ex"], env["row"]
            xc = X[:, bass.ds(k * QN, QN), :]
            step.link(v.tensor_scalar(z[:], z[:], 1e-16, None, ALU.add))
            step.link(v.reciprocal(z[:], z[:]))
            step.link(v.tensor_tensor(mix[:], mix[:], bcast(z[:], [P, QN, CH]), ALU.mult))
            v.tensor_tensor(mix[:], mix[:], bcast(b2_row[:].unsqueeze(1), [P, QN, CH]), ALU.add
                            ).then_inc(env["mid_ok"], 1)
            hold(dve, env["exp_ok"], k + 1)
            v.scalar_tensor_tensor(ex[:], ex[:], 1.0, pos[:], ALU.min, ALU.add).then_inc(env["flip_in"], 1)
            step.link(v.tensor_tensor(xc, xc, bcast(wf_const[:].unsqueeze(1), [P, QN, FEAT]), ALU.add))
            hold(dve, env["prod_ok"], k + 1)
            v.tensor_tensor(xc, xc, columns(env["ps_out"], FEAT), ALU.add).then_inc(env["used_ok"], 1)
            hold(dve, env["used_ok"], k + 2)
            layer_norm_relu(dve, step, xc, row[:, b], env["t"], QN, k).then_inc(env["row_ok"], 1)

        def d4_exp(env, b):
            nc.scalar.activation(env["pos"][:], env["mix"][:], ACT.Relu, scale=1.0 / SELU_ALPHA)
            return nc.scalar.activation(env["ex"][:], env["mix"][:], ACT.Exp)

        node_pass("d4", [acc2[0], acc2[1], t_gat2], t_rel1, FEAT, d4_prepare, d4_nodes, 4 + LN_LINKS,
                  flips=CH, wide=4 * FEAT, bd=bd_wf[:].rearrange("p j c -> p (j c)"), act_mid=d4_exp, prep_links=4)
        counts_ctx.close()

        def relation_messages(tag, F, ctx):
            rel = sb(f"{tag}_rel", [P, B], F32, ctx)
            inv = sb(f"{tag}_inv", [P, B], F32, ctx)
            hot = sb(f"{tag}_hot", [P, B, NREL], F32, ctx)

            def messages(dve, step, env, k, b, gathered):
                v = nc.vector
                cols = bass.ds(k * B, B)
                v.tensor_copy(inv[:], inv_cnt[:, cols])
                step.link(v.tensor_copy(rel[:], rel_f[:, cols]))
                step.link(v.tensor_tensor(hot[:], bcast(rel[:].unsqueeze(2), [P, B, NREL]),
                                          bcast(iota8[:].unsqueeze(1), [P, B, NREL]), ALU.is_equal))
                step.link(v.tensor_tensor(hot[:], hot[:], bcast(inv[:].unsqueeze(2), [P, B, NREL]), ALU.mult))
                hold(dve, *gathered)
                for s in range(B):
                    last = v.tensor_tensor(env["msg"][:, b, s].rearrange("p (r f) -> p r f", f=F),
                                           bcast(env["rings"][0][:, b, s].unsqueeze(1), [P, NREL, F]),
                                           bcast(hot[:, s].unsqueeze(2), [P, NREL, F]), ALU.mult)
                return last
            return messages

        with ExitStack() as ctx:
            scatter_pass("r1", [(t_rel1, src_i, FEAT)], key_dst, CH, acc3, relation_messages("r1m", FEAT, ctx), 3,
                         expand=1, weights=lambda a: rel_w1[:])

        def add_prepare(W):
            def prepare(what, pool, env, step, k, b):
                if what == "alloc":
                    new = dict(agg=env["tmp"]("agg", [P, QN, W]))
                    if len(env["ins"]) > 2:
                        new["flip_src"] = lambda b: env["ins"][2][:, b].rearrange("p q f -> p (q f)")
                    return new
                a0, a1 = env["ins"][0:2]
                step.link(nc.gpsimd.tensor_tensor(env["agg"][:], a0[:, b], a1[:, b], ALU.add))
            return prepare

        def d5_nodes(dve, env, step, k, b):
            v = nc.vector
            dve.sem_inc(env["flip_in"], 1)
            step.link(v.tensor_tensor(env["agg"][:], env["agg"][:], bcast(rb1_row[:].unsqueeze(1), [P, QN, CH]), ALU.add))
            hold(dve, env["prod_ok"], k + 1)
            step.link(v.tensor_tensor(env["agg"][:], env["agg"][:], columns(env["ps_out"], CH), ALU.add))
            step.link(v.tensor_scalar(env["row"][:, b], env["agg"][:], 0.0, None, ALU.max))
            dve.sem_inc(env["used_ok"], 1)
            dve.sem_inc(env["row_ok"], 1)

        node_pass("d5", [acc3[0], acc3[1], t_rel1], t_rel2, CH, add_prepare(CH), d5_nodes, 3, flips=FEAT,
                  wide=8 * CH, bd=bd_root1[:].rearrange("p j c -> p (j c)"), norm=False)

        with ExitStack() as ctx:
            scatter_pass("r2", [(t_rel2, src_i, CH)], key_dst, FEAT, acc4, relation_messages("r2m", CH, ctx), 3,
                         expand=2, weights=lambda a: rel_w2[:, a])

        def d6_nodes(dve, env, step, k, b):
            v = nc.vector
            xc = X[:, bass.ds(k * QN, QN), :]
            dve.sem_inc(env["flip_in"], 1)
            step.link(v.tensor_tensor(xc, xc, env["agg"][:], ALU.add))
            step.link(v.tensor_tensor(xc, xc, bcast(rb2_row[:].unsqueeze(1), [P, QN, FEAT]), ALU.add))
            hold(dve, env["prod_ok"], k + 1)
            step.link(v.tensor_tensor(xc, xc, columns(env["ps_out"], FEAT), ALU.add))
            dve.sem_inc(env["used_ok"], 1)
            layer_norm_relu(dve, step, xc, env["row"][:, b], env["t"], QN, k).then_inc(env["row_ok"], 1)

        node_pass("d6", [acc4[0], acc4[1], t_rel2], t_mix, FEAT, add_prepare(FEAT), d6_nodes, 3 + LN_LINKS, flips=CH,
                  wide=4 * FEAT, bd=bd_root2[:].rearrange("p j c -> p (j c)"))

        D_, E_, H_ = 5.0, 0.9, 0.1
        with ExitStack() as ctx:
            wts = sb("l2_wts", [P, B], F32, ctx)
            den = sb("l2_den", [P, B, FEAT], F32, ctx)
            num = sb("l2_num", [P, B, FEAT], F32, ctx)

            def l2_messages(dve, step, env, k, b, gathered):
                v = nc.vector
                xi, xj = (r[:, b] for r in env["rings"])
                v.tensor_copy(wts[:], weight[:, bass.ds(k * B, B)])
                hold(dve, *gathered)
                step.link(v.tensor_scalar(den[:], xi, E_, D_, ALU.mult, ALU.add))
                step.link(v.scalar_tensor_tensor(den[:], xj, H_, den[:], ALU.mult, ALU.add))
                step.link(v.reciprocal(den[:], den[:]))
                step.link(v.tensor_tensor(num[:], xi, bcast(wts[:].unsqueeze(2), [P, B, FEAT]), ALU.mult))
                step.link(v.tensor_tensor(num[:], num[:], xj, ALU.mult))
                return v.tensor_tensor(env["msg"][:, b], num[:], den[:], ALU.mult)

            scatter_pass("l2", [(t_mix, src_i, FEAT), (t_mix, dst_i, FEAT)], key_src, FEAT, acc5, l2_messages, 5)

        v_dst = sb("v_dst", [P, C])

        def d7_prepare(what, pool, env, step, k, b):
            if what == "alloc":
                return dict(agg=env["tmp"]("agg", [P, QN, FEAT]), u=env["tmp"]("u", [P, QN, FEAT]))
            g = nc.gpsimd
            a0, a1, h = env["ins"]
            step.link(g.tensor_scalar(env["u"][:], h[:, b], -1.0 / 5.0, 1.0, ALU.mult, ALU.add))
            step.link(g.tensor_tensor(env["agg"][:], a0[:, b], a1[:, b], ALU.add))
            step.link(g.tensor_tensor(env["u"][:], env["u"][:], h[:, b], ALU.mult))

        def d7_nodes(dve, env, step, k, b):
            v = nc.vector
            h, u, agg, row = env["ins"][2], env["u"], env["agg"], env["row"]
            cols = bass.ds(k * QN, QN)
            xc = X[:, cols, :]
            step.link(v.tensor_tensor(xc, xc, agg[:], ALU.add))
            step.link(v.scalar_tensor_tensor(u[:], h[:, b], -1.0, u[:], ALU.add, ALU.mult))
            step.link(v.scalar_tensor_tensor(xc, u[:], 0.1, xc, ALU.add, ALU.add))
            dve.sem_inc(env["used_ok"], 1)
            step.link(layer_norm_relu(dve, step, xc, row[:, b], env["t"], QN, k))
            step.link(v.tensor_tensor(env["t"]["cent"][:], row[:, b], bcast(c_row[:, 2:3, :], [P, QN, FEAT]), ALU.mult))
            v.tensor_reduce(v_dst[:, cols], env["t"]["cent"][:], AX_X, ALU.add).then_inc(env["row_ok"], 1)

        node_pass("d7", [acc5[0], acc5[1], t_mix], t_last, FEAT, d7_prepare, d7_nodes, 5 + LN_LINKS, prep_links=3)

        with ExitStack() as ctx:
            attr = sb("attr", [P, T, FEAT], F32, ctx)
            wide_t = sb("wide_t", [P, B, FEAT, FEAT], F32, ctx)
            part = sb("l3_part", [P, B, FEAT], F32, ctx)
            mrow = sb("l3_mrow", [P, B, FEAT], F32, ctx)
            u = sb("l3_u", [P, B], F32, ctx)
            u2 = sb("l3_u2", [P, B], F32, ctx)
            a_s, c_s = semaphore(ctx, "attr_in"), semaphore(ctx, "attr_clear")
            with nc.Block() as block:
                @block.vector
                def _(dve):
                    nc.vector.memset(attr[96:P], 0.0).then_inc(c_s, 1)

                @block.sync
                def _(sp):
                    sp.wait_ge(c_s, 1)
                    sp.dma_start(attr[0:EP], edge_attr_16[0:EP * T].rearrange("(p t) f -> p t f", t=T)).then_inc(a_s, 16)
                    sp.dma_start(attr[EP:EP + 1, 0:EREST], edge_attr_16[EP * T:E].rearrange("(p t) f -> p t f", p=1)
                                 ).then_inc(a_s, 16)
                    sp.wait_ge(a_s, 32)

            def l3_messages(dve, step, env, k, b, gathered):
                v = nc.vector
                h = env["rings"][0][:, b]
                msg = env["msg"]
                v.tensor_scalar(env["pick"][:], env["typs"][:, b], lane[:], None, ALU.is_equal
                                ).then_inc(env["pick_ok"], 1)
                step.link(v.tensor_tensor(part[:], attr[:, bass.ds(k * B, B), :], bcast(c_row[:, 1:2, :], [P, B, FEAT]),
                                          ALU.mult))
                step.link(v.tensor_reduce(u2[:], part[:], AX_X, ALU.add))
                hold(dve, *gathered)
                step.link(v.tensor_tensor(part[:], h, bcast(c_row[:, 0:1, :], [P, B, FEAT]), ALU.mult))
                step.link(v.tensor_reduce(u[:], part[:], AX_X, ALU.add))
                step.link(v.tensor_tensor(u[:], u[:], u2[:], ALU.add))
                hold(dve, env["mats_ok"], k + 1)
                for s in range(B):
                    last = v.tensor_tensor(wide_t[:, s], env["ps_mid"][:, 256 * s:256 * (s + 1)].rearrange(
                        "p (i o) -> p i o", o=FEAT), bcast(h[:, s].unsqueeze(2), [P, FEAT, FEAT]), ALU.mult)
                step.link(last)
                step.link(v.tensor_reduce(mrow[:], wide_t[:].rearrange("p s i o -> p s o i"), AX_X, ALU.add))
                v.tensor_copy(msg[:, b, :, FEAT:2 * FEAT], mrow[:])
                return v.tensor_tensor(msg[:, b, :, 0:FEAT], mrow[:], bcast(u[:].unsqueeze(2), [P, B, FEAT]), ALU.mult)

            scatter_pass("l3", [(t_last, src_i, FEAT)], key_dst, 2 * FEAT, acc6, l3_messages, 7, extra=True)

        def d8_nodes(dve, env, step, k, b):
            v = nc.vector
            agg, row, u = env["agg"], env["row"], env["u"]
            cols = bass.ds(k * QN, QN)
            step.link(v.tensor_tensor(agg[:, :, FEAT:2 * FEAT], agg[:, :, FEAT:2 * FEAT],
                                      bcast(v_dst[:, cols].unsqueeze(2), [P, QN, FEAT]), ALU.mult))
            step.link(v.tensor_tensor(u[:], agg[:, :, FEAT:2 * FEAT], agg[:, :, 0:FEAT], ALU.add))
            dve.sem_inc(env["used_ok"], 1)
            step.link(v.tensor_tensor(X[:, cols, :], X[:, cols, :], u[:], ALU.add))
            dve.sem_inc(env["row_ok"], 1)

        def d8_prepare(what, pool, env, step, k, b):
            if what == "alloc":
                return dict(agg=env["tmp"]("agg", [P, QN, 2 * FEAT]), u=env["tmp"]("u", [P, QN, FEAT]))
            a0, a1 = env["ins"]
            step.link(nc.gpsimd.tensor_tensor(env["agg"][:], a0[:, b], a1[:, b], ALU.add))

        node_pass("d8", [acc6[0], acc6[1]], None, FEAT, d8_prepare, d8_nodes, 3, norm=False)
        with ExitStack() as ctx:
            o_s = semaphore(ctx, "final")
            with nc.Block() as block:
                @block.sync
                def _(sp):
                    sp.dma_start(out.rearrange("(p c) f -> p c f", c=C), X[0:NPART]).then_inc(o_s, 16)
                    sp.wait_ge(o_s, 16)


INPUTS = ["x", "src", "dst", "edge_attr_16", "edge_type_8", "edge_type_90", "edge_weight",
          "L0_gnn_W1", "L0_gnn_a_src1", "L0_gnn_a_dst1", "L0_gnn_b1", "L0_gnn_W2", "L0_gnn_a_src2", "L0_gnn_a_dst2",
          "L0_gnn_b2", "L0_gnn_Wf", "L0_gnn_bf", "L1_gnn_W1", "L1_gnn_root1", "L1_gnn_b1", "L1_gnn_W2",
          "L1_gnn_root2", "L1_gnn_b2", "L3_gnn_Ws", "L3_gnn_Wa", "L3_gnn_weight", "L3_gnn_w_comp"]


def kernel(**inputs):
    import numpy as np
    import concourse.bacc as bacc
    from concourse.bass_utils import run_bass_kernel_spmd

    nc = bacc.Bacc("TRN2", target_bir_lowering=False, num_devices=1)
    arrays, args = {}, []
    for name in INPUTS:
        a = np.ascontiguousarray(inputs[name])
        arrays[f"in_{name}"] = a
        args.append(nc.dram_tensor(f"in_{name}", a.shape, mybir.dt.from_np(a.dtype), kind="ExternalInput").ap())
    shape = inputs["x"].shape
    args.append(nc.dram_tensor("out_0", tuple(shape), F32, kind="ExternalOutput").ap())
    gnn_kernel(nc, *args)
    r = run_bass_kernel_spmd(nc, [arrays], core_ids=[0])
    return r.results[0]["out_0"]
```

```python
from contextlib import ExitStack

import concourse.bass as bass
from concourse import mybir

ALU = mybir.AluOpType
ACT = mybir.ActivationFunctionType
F32 = mybir.dt.float32
I32 = mybir.dt.int32
AX_X = mybir.AxisListType.X

P = 128
FEAT = 16
HEADS1, CH = 3, 32
HID = HEADS1 * CH
NREL, RELS, BASES = 8, 90, 30

B = 7
C = 800

SLOPE = 0.2
EPS = 1e-5
SELU_ALPHA = 1.6732632423543772
SELU_SCALE = 1.0507009873554805
FAR = -1e30
WIDTH1 = HEADS1 * FEAT + HEADS1 + NREL
WIDTH2 = CH + 1


class Steps:

    def __init__(self, engine, sem, base=0, apart=False):
        self.engine, self.sem, self.base, self.n, self.apart = engine, sem, base, 0, apart

    def link(self, instruction):
        self.n += 1
        instruction.then_inc(self.sem, 1)
        self.engine.wait_ge(self.sem, self.base + self.n)
        if self.apart:
            self.engine.nop(nofuse=True)


def hold(engine, sem, value):
    engine.wait_ge(sem, value)
    engine.nop(nofuse=True)


def each_chunk(engine, half, body):
    with engine.Fori(0, half - 1) as i:
        body(i, 0, (i, 1), (i + 1, 0))
        body(i, 1, (i + 1, 0), (i + 1, 1))
    body(half - 1, 0, (half - 1, 1), None)
    body(half - 1, 1, None, None)


def bcast(ap, shape):
    return ap.broadcast_to(shape)


def gnn_kernel(nc, x, src, dst, edge_attr_16, edge_type_8, edge_type_90, edge_weight,
               W1, a_src1, a_dst1, b1, W2, a_src2, a_dst2, b2, Wf, bf,
               RW1, root1, rb1, RW2, root2, rb2, Ws, Wa, bases, w_comp, out):
    N = x.shape[0]
    E = src.shape[0]
    T = -(-E // (P * 2 * B)) * 2 * B
    ITER = T // (2 * B)
    EP = E // T
    EREST = E - EP * T
    NPART = N // C
    NP = P * C
    assert EP == P - 1 and NPART * C == N and NP - N >= P
    AHEAD = 2 * B

    def scratch(name, shape, dt=F32):
        return nc.dram_tensor(name, shape, dt, kind="Internal").ap()

    t_gat1 = scratch("t_gat1", (NP, FEAT + HEADS1))
    t_norm1 = scratch("t_norm1", (NP, 2 * HEADS1))
    t_gat2 = scratch("t_gat2", (NP, CH + 1))
    t_norm2 = scratch("t_norm2", (NP, 2 + NREL))
    t_rel1 = scratch("t_rel1", (NP, FEAT))
    t_rel2 = scratch("t_rel2", (NP, CH))
    t_mix = scratch("t_mix", (NP, FEAT))
    t_last = scratch("t_last", (NP, FEAT))
    max1 = [scratch(f"max1_{s}", (NP, HEADS1)) for s in range(B)]
    max2 = [scratch(f"max2_{s}", (NP, 1)) for s in range(B)]
    acc1 = [scratch(f"acc1_{r}", (NP, WIDTH1)) for r in range(2)]
    acc2 = [scratch(f"acc2_{r}", (NP, WIDTH2)) for r in range(2)]
    acc3 = [scratch(f"acc3_{r}", (NP, CH)) for r in range(2)]
    acc4 = [scratch(f"acc4_{r}", (NP, FEAT)) for r in range(2)]
    acc5 = [scratch(f"acc5_{r}", (NP, FEAT)) for r in range(2)]
    acc6 = [scratch(f"acc6_{r}", (NP, 2 * FEAT)) for r in range(2)]
    row_src = scratch("row_src", (T, P))
    row_dst = scratch("row_dst", (T, P))
    row_typ = scratch("row_typ", (T, P))
    w_rel_dram = scratch("w_rel_dram", (RELS * FEAT, FEAT))
    primer = scratch("primer", (P, 4))

    def by_node(table):
        return table.rearrange("(p c) f -> p c f", p=P)

    def flat(table):
        return table.rearrange("(p c) f -> p (c f)", p=P)

    in_phase = {}

    def semaphore(ctx, name):
        if id(ctx) not in in_phase:
            in_phase[id(ctx)] = []
            ctx.callback(clear, id(ctx))
        in_phase[id(ctx)].append(nc.alloc_semaphore(name))
        return in_phase[id(ctx)][-1]

    def clear(phase):
        nc.clear_and_free_semaphores(in_phase.pop(phase))
        nc.all_engine_barrier()

    with ExitStack() as top:
        def sb(name, shape, dt=F32, ctx=top):
            return ctx.enter_context(nc.sbuf_tensor(name, shape, dt))

        X = sb("X", [P, C, FEAT])
        src_i = sb("src_i", [P, T + AHEAD], I32)
        dst_i = sb("dst_i", [P, T + AHEAD], I32)
        src_f = sb("src_f", [P, T])
        dst_f = sb("dst_f", [P, T])
        rel_f = sb("rel_f", [P, T])
        weight = sb("weight", [P, T])
        inv_cnt = sb("inv_cnt", [P, T])
        uniq_dst = sb("uniq_dst", [P, T], I32)
        uniq_src = sb("uniq_src", [P, T], I32)
        ident = sb("ident", [P, P])
        earlier = sb("earlier", [P, P])
        iota8 = sb("iota8", [P, NREL])
        lane = sb("lane", [P, 1])
        spare = sb("spare", [P, 1])
        bd_score = sb("bd_score", [P, 8, 2 * HEADS1])
        w1_half = sb("w1_half", [HID, 2, HEADS1, CH])
        b1_col = sb("b1_col", [HID, 2])
        w2_ext = sb("w2_ext", [HID, CH + 2])
        w2_const = sb("w2_const", [P, CH + 2])
        bd_wf = sb("bd_wf", [P, 4, FEAT])
        wf_const = sb("wf_const", [P, FEAT])
        b2_row = sb("b2_row", [P, CH])
        rel_w1 = sb("rel_w1", [P, CH])
        rel_w2 = sb("rel_w2", [P, 2, FEAT])
        bd_root1 = sb("bd_root1", [P, 8, CH])
        bd_root2 = sb("bd_root2", [P, 4, FEAT])
        rb1_row = sb("rb1_row", [P, CH])
        rb2_row = sb("rb2_row", [P, FEAT])
        c_row = sb("c_row", [P, 3, FEAT])
        w_rel = sb("w_rel", [P, FEAT, FEAT])
        primed = sb("primed", [P, 4])

        def psum_all(ctx, name):
            return ctx.enter_context(nc.psum_tensor(name, [P, 8 * 512], F32))

        with ExitStack() as ctx:
            def tmp(name, shape, dt=F32):
                return sb(name, shape, dt, ctx)

            def sem(name):
                return semaphore(ctx, name)

            rel_i = tmp("rel_i", [P, T], I32)
            typ_i = tmp("typ_i", [P, T], I32)
            typ_f = tmp("typ_f", [P, T])
            w1_rep = tmp("w1_rep", [P, HID])
            a1_rep = tmp("a1_rep", [P, 2, HID])
            prod1 = tmp("prod1", [P, 2, HID])
            score1 = tmp("score1", [P, 2 * HEADS1])
            w2_raw = tmp("w2_raw", [HID, CH])
            a2_rep = tmp("a2_rep", [HID, 2, CH])
            prod2 = tmp("prod2", [HID, 2, CH])
            wf_rep = tmp("wf_rep", [P, FEAT])
            bf_row = tmp("bf_row", [P, FEAT])
            root1_rep = tmp("root1_rep", [P, CH])
            root2_rep = tmp("root2_rep", [P, FEAT])
            mask8 = tmp("mask8", [P, 8])
            mask4 = tmp("mask4", [P, 4])
            ones = tmp("ones", [P, P])
            ws_sb = tmp("ws_sb", [FEAT, FEAT])
            wa_sb = tmp("wa_sb", [FEAT, 3])
            wa_wide = tmp("wa_wide", [FEAT, 3, P])
            basis = tmp("basis", [BASES, FEAT, FEAT])
            comp_t = tmp("comp_t", [BASES, RELS])
            w_flat = tmp("w_flat", [RELS, FEAT, FEAT])
            QT = T // 4
            rows = tmp("rows", [QT, 3, 4, P])
            ps = psum_all(ctx, "ps_setup")
            s_cleared = sem("s_cleared")
            s_masks = sem("s_masks")
            s_loaded = sem("s_loaded")
            s_float = sem("s_float")
            s_step = sem("s_step")
            s_rows_t = sem("s_rows_t")
            s_rows = sem("s_rows")
            s_wts = sem("s_wts")
            s_prods = sem("s_prods")
            s_flat = sem("s_flat")
            s_stored = sem("s_stored")
            s_back = sem("s_back")
            s_edges = sem("s_edges")
            s_x = sem("s_x")
            n_loads = [0]
            with nc.Block() as block:
                @block.sync
                def _(sp):
                    def load(to, frm):
                        sp.dma_start(to, frm).then_inc(s_loaded, 16)
                        n_loads[0] += 1

                    for j in range(8):
                        load(w1_rep[FEAT * j:FEAT * (j + 1), :], W1)
                        load(root1_rep[FEAT * j:FEAT * (j + 1), :], root1)
                    for j in range(4):
                        load(wf_rep[CH * j:CH * (j + 1), :], Wf)
                        load(root2_rep[CH * j:CH * (j + 1), :], root2)
                    load(a1_rep[:, 0, :], a_src1.rearrange("h c -> (h c)").partition_broadcast(P))
                    load(a1_rep[:, 1, :], a_dst1.rearrange("h c -> (h c)").partition_broadcast(P))
                    load(a2_rep[:, 0, :], a_src2.rearrange("h c -> (h c)").partition_broadcast(HID))
                    load(a2_rep[:, 1, :], a_dst2.rearrange("h c -> (h c)").partition_broadcast(HID))
                    load(w2_raw[:], W2)
                    load(b1_col[:, 0:1], b1.rearrange("(c o) -> c o", o=1))
                    load(bf_row[:], bf.partition_broadcast(P))
                    load(b2_row[:], b2.partition_broadcast(P))
                    load(rb1_row[:], rb1.partition_broadcast(P))
                    load(rb2_row[:], rb2.partition_broadcast(P))
                    load(rel_w1[:], RW1.rearrange("r f c -> (r f) c"))
                    load(rel_w2[:], RW2.rearrange("(a r) f c -> (r f) a c", a=2))
                    load(ws_sb[:], Ws)
                    with nc.allow_non_contiguous_dma(reason="small transposed weights"):
                        load(wa_sb[:], Wa.rearrange("a (k o) -> o (a k)", k=3))
                        load(comp_t[:], w_comp.rearrange("r b -> b r"))
                    load(basis[:], bases.rearrange("b i o -> (b i o)").rearrange("(i b o) -> b i o", b=BASES, o=FEAT))
                    sp.wait_ge(s_rows, 3)
                    for n, table in enumerate((row_src, row_dst, row_typ)):
                        sp.dma_start(table.rearrange("(k q) p -> q k p", q=QT), rows[:, n]).then_inc(s_stored, 16)
                    sp.wait_ge(s_flat, 1)
                    sp.dma_start(w_rel_dram.rearrange("(i r) o -> r i o", r=RELS), w_flat[:]).then_inc(s_stored, 16)
                    sp.wait_ge(s_stored, 64)
                    sp.dma_start(w_rel[0:RELS], w_rel_dram.rearrange("(r i) o -> r i o", i=FEAT)).then_inc(s_back, 16)
                    sp.wait_ge(s_back, 16)
                    sp.wait_ge(s_loaded, 16 * n_loads[0])

                n_edges = 16 * 10
                n_in = 16 * (16 + 8 + 4 + 1 + 1 + 4 + 2 + 1 + 2 + 1)

                @block.gpsimd
                def _(pool):
                    step = Steps(pool, s_masks)
                    g = nc.gpsimd
                    step.link(g.memset(ident[:], 0.0))
                    step.link(g.affine_select(out=ident[:], in_=ident[:], compare_op=ALU.not_equal, fill=1.0, base=0,
                                              pattern=[[-1, P]], channel_multiplier=1))
                    step.link(g.memset(earlier[:], 1.0))
                    step.link(g.affine_select(out=earlier[:], in_=earlier[:], compare_op=ALU.is_ge, fill=0.0, base=-1,
                                              pattern=[[-1, P]], channel_multiplier=1))
                    step.link(g.memset(ones[:], 1.0))
                    for mask, n, w in ((mask8, 8, 16), (mask4, 4, 32)):
                        step.link(g.memset(mask[:], 1.0))
                        step.link(g.affine_select(out=mask[:], in_=mask[:], compare_op=ALU.is_ge, fill=0.0, base=0,
                                                  pattern=[[-w, n]], channel_multiplier=1))
                        step.link(g.affine_select(out=mask[:], in_=mask[:], compare_op=ALU.is_ge, fill=0.0,
                                                  base=w - 1, pattern=[[w, n]], channel_multiplier=-1))
                    step.link(g.iota(lane[:], pattern=[[0, 1]], base=0, channel_multiplier=1,
                                     allow_small_or_imprecise_dtypes=True))
                    step.link(g.iota(spare[:], pattern=[[0, 1]], base=N, channel_multiplier=1,
                                     allow_small_or_imprecise_dtypes=True))
                    step.link(g.iota(iota8[:], pattern=[[1, NREL]], base=0, channel_multiplier=0,
                                     allow_small_or_imprecise_dtypes=True))

                n_masks = 14

                @block.vector
                def _(dve):
                    v = nc.vector
                    step = Steps(dve, s_step)
                    v.memset(src_i[:], N + P - 1)
                    v.memset(dst_i[:], N + P - 1)
                    v.memset(rel_i[:], 0)
                    v.memset(typ_i[:], 0)
                    v.memset(weight[:], 0.0)
                    v.memset(w_rel[:], 0.0)
                    v.memset(primed[:], 0.0)
                    v.memset(X[96:P, :, :], 0.0).then_inc(s_cleared, 1)
                    dve.wait_ge(s_edges, n_edges)
                    v.tensor_copy(src_f[:], src_i[:, 0:T])
                    v.tensor_copy(dst_f[:], dst_i[:, 0:T])
                    v.tensor_copy(typ_f[:], typ_i[:]).then_inc(s_float, 1)
                    v.tensor_copy(rel_f[:], rel_i[:])
                    dve.wait_ge(s_masks, n_masks)
                    dve.wait_ge(s_loaded, n_in)
                    step.link(v.tensor_tensor(prod1[:], bcast(w1_rep[:].unsqueeze(1), [P, 2, HID]), a1_rep[:],
                                              ALU.mult))
                    step.link(v.tensor_reduce(score1[:].rearrange("p (k h) -> p k h", k=2),
                                              prod1[:].rearrange("p k (h c) -> p k h c", c=CH), AX_X, ALU.add))
                    v.tensor_tensor(bd_score[:], bcast(score1[:].unsqueeze(1), [P, 8, 2 * HEADS1]),
                                    bcast(mask8[:].unsqueeze(2), [P, 8, 2 * HEADS1]), ALU.mult)
                    v.tensor_tensor(bd_root1[:], bcast(root1_rep[:].unsqueeze(1), [P, 8, CH]),
                                    bcast(mask8[:].unsqueeze(2), [P, 8, CH]), ALU.mult)
                    v.tensor_tensor(bd_root2[:], bcast(root2_rep[:].unsqueeze(1), [P, 4, FEAT]),
                                    bcast(mask4[:].unsqueeze(2), [P, 4, FEAT]), ALU.mult)
                    for j in range(2):
                        v.tensor_tensor(w1_half[:, j], w1_rep[0:HID, :].rearrange("p (h c) -> p h c", c=CH),
                                        bcast(mask8[0:HID, 3 * j:3 * j + 3].unsqueeze(2), [HID, HEADS1, CH]), ALU.mult)
                    v.tensor_scalar(b1_col[:, 1:2], b1_col[:, 0:1], 1.0 / SELU_ALPHA, None, ALU.mult)
                    v.tensor_scalar(w2_ext[:, 0:CH], w2_raw[:], SELU_SCALE * SELU_ALPHA, None, ALU.mult)
                    step.link(v.tensor_scalar(wf_rep[:], wf_rep[:], SELU_SCALE * SELU_ALPHA, None, ALU.mult))
                    step.link(v.tensor_tensor(prod2[:], bcast(w2_ext[:, 0:CH].unsqueeze(1), [HID, 2, CH]), a2_rep[:],
                                              ALU.mult))
                    v.tensor_reduce(w2_ext[:, CH:CH + 2], prod2[:], AX_X, ALU.add)
                    v.tensor_tensor(bd_wf[:], bcast(wf_rep[:].unsqueeze(1), [P, 4, FEAT]),
                                    bcast(mask4[:].unsqueeze(2), [P, 4, FEAT]), ALU.mult)
                    for k in range(3):
                        last = v.tensor_scalar(wa_wide[:, k], ones[0:FEAT, :], wa_sb[:, k:k + 1], None, ALU.mult)
                    last.then_inc(s_wts, 1)
                    dve.wait_ge(s_prods, 1)
                    v.tensor_scalar(w2_const[:], ps[:, 1536:1536 + CH + 2], -1.0, None, ALU.mult)
                    v.tensor_tensor(wf_const[:], bf_row[:], ps[:, 1600:1600 + FEAT], ALU.subtract)
                    v.tensor_copy(c_row[:].rearrange("p k f -> p (k f)"), ps[:, 1664:1664 + 3 * FEAT])

                @block.tensor
                def _(pe):
                    pe.wait_ge(s_masks, n_masks)
                    pe.wait_ge(s_float, 1)
                    for n, rows_f in enumerate((src_f, dst_f, typ_f)):
                        for k in range(4):
                            col = 512 * n + P * k
                            last = nc.tensor.transpose(ps[0:QT, col:col + P], rows_f[:, QT * k:QT * (k + 1)], ident[:])
                        last.then_inc(s_rows_t, 1)
                    pe.wait_ge(s_wts, 1)
                    nc.tensor.matmul(ps[:, 1536:1536 + CH + 2], ones[0:HID, :], w2_ext[:], start=True, stop=True)
                    nc.tensor.matmul(ps[:, 1600:1600 + FEAT], ones[0:CH, :], wf_rep[0:CH, :], start=True, stop=True)
                    for k in range(3):
                        col = 1664 + FEAT * k
                        nc.tensor.matmul(ps[:, col:col + FEAT], wa_wide[:, k], ws_sb[:], start=True, stop=True)
                    nc.tensor.matmul(ps[0:RELS, 2048:2048 + FEAT * FEAT], comp_t[:],
                                     basis[:].rearrange("b i o -> b (i o)"), start=True, stop=True).then_inc(s_prods, 1)

                @block.scalar
                def _(act):
                    act.wait_ge(s_cleared, 1)
                    for to, frm in ((src_i, src), (dst_i, dst), (rel_i, edge_type_8), (typ_i, edge_type_90),
                                    (weight, edge_weight)):
                        act.dma_start(to[0:EP, 0:T], frm[0:EP * T].rearrange("(p t) -> p t", t=T)).then_inc(s_edges, 16)
                        act.dma_start(to[EP:EP + 1, 0:EREST], frm[EP * T:E].rearrange("(p t) -> p t", p=1)
                                      ).then_inc(s_edges, 16)
                    act.dma_start(X[0:NPART, :, :], x.rearrange("(p c) f -> p c f", c=C)).then_inc(s_x, 16)
                    for n in range(3):
                        act.wait_ge(s_rows_t, n + 1)
                        nc.scalar.copy(rows[:, n], ps[0:QT, 512 * n:512 * (n + 1)].rearrange("q (k p) -> q k p", p=P)
                                       ).then_inc(s_rows, 1)
                    act.wait_ge(s_prods, 1)
                    nc.scalar.copy(w_flat[:], ps[0:RELS, 2048:2048 + FEAT * FEAT].rearrange("r (i o) -> r i o", o=FEAT)
                                   ).then_inc(s_flat, 1)
                    act.wait_ge(s_x, 16)

        def ln_front(step, rows_in, t, k):
            v = nc.vector
            step.link(v.tensor_reduce(t["sum"][:], rows_in, AX_X, ALU.add))
            step.link(v.scalar_tensor_tensor(t["cent"][:], bcast(t["sum"][:].unsqueeze(2), rows_in.shape), -1.0 / FEAT,
                                             rows_in, ALU.mult, ALU.add))
            step.link(v.tensor_tensor(t["sq"][:], t["cent"][:], t["cent"][:], ALU.mult))
            step.link(v.tensor_reduce(t["var"][:], t["sq"][:], AX_X, ALU.add))
            v.tensor_scalar(t["var"][:], t["var"][:], 1.0 / FEAT, EPS, ALU.mult, ALU.add).then_inc(t["var_ok"], 1)

        def ln_back(dve, step, rows_out, t, k):
            v = nc.vector
            hold(dve, t["root_ok"], k + 1)
            step.link(v.reciprocal(t["root"][:], t["root"][:]))
            return v.scalar_tensor_tensor(rows_out, t["cent"][:], 0.0, bcast(t["root"][:].unsqueeze(2), rows_out.shape),
                                          ALU.max, ALU.mult)

        LN_FRONT, LN_BACK = 4, 1

        def take_root(act, t, k):
            hold(act, t["var_ok"], k + 1)
            nc.scalar.activation(t["root"][:], t["var"][:], ACT.Sqrt).then_inc(t["root_ok"], 1)

        def ln_buffers(ctx, q, tag):
            return {"sum": sb(f"{tag}_ln_sum", [P, q], F32, ctx), "cent": sb(f"{tag}_ln_cent", [P, q, FEAT], F32, ctx),
                    "sq": sb(f"{tag}_ln_sq", [P, q, FEAT], F32, ctx), "var": sb(f"{tag}_ln_var", [P, q], F32, ctx),
                    "root": sb(f"{tag}_ln_root", [P, q], F32, ctx),
                    "var_ok": semaphore(ctx, f"{tag}_var_ok"),
                    "root_ok": semaphore(ctx, f"{tag}_root_ok")}

        counts_ctx = ExitStack()
        counts = sb("counts", [P, C, NREL], F32, counts_ctx)
        as2 = sb("as2", [P, C, 1], F32, counts_ctx)
        ad2 = sb("ad2", [P, C, 1], F32, counts_ctx)
        self2 = sb("self2", [P, C, 1], F32, counts_ctx)
        gat = ExitStack()
        as1 = sb("as1", [P, C, HEADS1], F32, gat)
        ad1 = sb("ad1", [P, C, HEADS1], F32, gat)
        self1 = sb("self1", [P, C, HEADS1], F32, gat)

        with ExitStack() as ctx:
            def sem(name):
                return semaphore(ctx, name)

            Q = 80
            HALF = C // Q // 2
            t = [ln_buffers(ctx, Q, f"d0_{b}") for b in range(2)]
            row = sb("row", [P, 2, Q, FEAT + HEADS1], F32, ctx)
            h_c = sb("h_c", [P, 2, Q * FEAT], F32, ctx)
            h_t = sb("h_t", [P, 2, Q * FEAT], F32, ctx)
            ps = psum_all(ctx, "ps_h0")
            step_s = sem("step_s")
            norm_done, flip_done, copy_done, prod_done, out_done = (sem(n) for n in (
                "norm_done", "flip_done", "copy_done", "prod_done", "out_done"))
            store = [sem("store0"), sem("store1")]
            m_done = sem("m_done")
            COLS = Q * FEAT
            OUT = 2 * COLS
            NG = COLS // P
            assert OUT % 512 == 0 and 48 * NG <= 512
            with nc.Block() as block:
                @block.vector
                def _(dve):
                    v = nc.vector

                    def start(i, b, step):
                        ln_front(step, X[:, bass.ds((i * 2 + b) * Q, Q), :], t[b], i)

                    def body(i, b, following, _):
                        k = i * 2 + b
                        step = Steps(dve, step_s, LN_FRONT + k * (LN_FRONT + LN_BACK + 1))
                        if following:
                            start(*following, step)
                        hold(dve, store[b], i * 16 + 16)
                        hold(dve, copy_done, k + 1)
                        normed = h_c[:, b].rearrange("p (q f) -> p q f", f=FEAT)
                        step.link(ln_back(dve, step, normed, t[b], i))
                        v.tensor_copy(row[:, b, :, 0:FEAT], normed).then_inc(norm_done, 1)

                    start(0, 0, Steps(dve, step_s))
                    each_chunk(dve, HALF, body)

                @block.tensor
                def _(pe):
                    pe.sem_inc(flip_done, 2)
                    with pe.Fori(0, HALF) as i:
                        for b in range(2):
                            k = i * 2 + b
                            hold(pe, norm_done, k + 1)
                            hold(pe, copy_done, k + 1)
                            for g in range(NG):
                                last = nc.tensor.transpose(ps[:, COLS * b + P * g:COLS * b + P * (g + 1)],
                                                           h_c[:, b, P * g:P * (g + 1)], ident[:])
                            last.then_inc(flip_done, 1)
                            hold(pe, copy_done, k + 3)
                            hold(pe, out_done, k + 1)
                            for g in range(NG):
                                col = OUT + 512 * b + 48 * g
                                last = nc.tensor.matmul(ps[:, col:col + 48], h_t[:, b, P * g:P * (g + 1)],
                                                        bd_score[:].rearrange("p j s -> p (j s)"), start=True, stop=True)
                            last.then_inc(prod_done, 1)

                @block.scalar
                def _(act):
                    act.sem_inc(copy_done, 2)
                    act.sem_inc(out_done, 2)
                    with act.Fori(0, HALF) as i:
                        for b in range(2):
                            k = i * 2 + b
                            take_root(act, t[b], i)
                            hold(act, flip_done, k + 3)
                            nc.scalar.copy(h_t[:, b], ps[:, COLS * b:COLS * (b + 1)]).then_inc(copy_done, 1)
                            hold(act, prod_done, k + 1)
                            view = ps[:, OUT + 512 * b:OUT + 512 * b + 6 * Q].rearrange("p (q s) -> p q s", s=6)
                            nc.scalar.copy(row[:, b, :, FEAT:FEAT + HEADS1], view[:, :, 0:HEADS1])
                            nc.scalar.copy(as1[:, bass.ds(k * Q, Q), :], view[:, :, 0:HEADS1])
                            nc.scalar.copy(ad1[:, bass.ds(k * Q, Q), :], view[:, :, HEADS1:2 * HEADS1]
                                           ).then_inc(out_done, 1)

                @block.sync
                def _(sp):
                    for b in range(2):
                        sp.dma_start(primer, primed[:]).then_inc(store[b], 16)
                        sp.wait_ge(store[b], 16)
                    with sp.Fori(0, HALF) as i:
                        for b in range(2):
                            k = i * 2 + b
                            hold(sp, out_done, k + 3)
                            sp.dma_start(by_node(t_gat1)[:, bass.ds(k * Q, Q), :], row[:, b]).then_inc(store[b], 16)
                    sp.wait_ge(out_done, 2 * HALF + 2)
                    for table in max1:
                        sp.dma_start(by_node(table), as1[:]).then_inc(m_done, 16)
                    sp.wait_ge(m_done, 16 * B)
                    for b in range(2):
                        sp.wait_ge(store[b], 16 * (HALF + 1))

        def segment_max(tag, table, replicas, H, F, keep, first):
            W = F + H
            with ExitStack() as ctx:
                def tmp(name, shape, dt=F32):
                    return sb(f"{tag}_{name}", shape, dt, ctx)

                def sem(name):
                    return semaphore(ctx, f"{tag}_{name}")

                rowd = tmp("rowd", [P, 2, B, P])
                rows_ = tmp("rows", [P, 2, B, P]) if first else None
                ring = tmp("ring", [P, 2, B, W])
                cur = tmp("cur", [P, 2, B, H])
                new = tmp("new", [P, 2, B, H])
                st_g, st_d, st_u = (tmp(n, [P, 2, B], I32) for n in ("st_g", "st_d", "st_u"))
                own = tmp("own", [P, 2, B])
                pen = tmp("pen", [P, B, P])
                lone = tmp("lone", [P, B, P])
                reps = tmp("reps", [P, 2, B])
                part = tmp("part", [P, 2, B])
                masked = tmp("masked", [P, B, H, P])
                group = tmp("group", [P, B, H])
                ps = psum_all(ctx, f"{tag}_ps")
                pv = ps[:, 0:B * 512].rearrange("p (s z) -> p s z", z=512)
                rows_in = [sem("rows_in0"), sem("rows_in1")]
                rows_free = sem("rows_free")
                gat_in = [sem("gat_in0"), sem("gat_in1")]
                cur_in = [sem("cur_in0"), sem("cur_in1")]
                kept = sem("kept")
                masked_ok = sem("masked_ok")
                flipped = sem("flipped")
                new_ok = sem("new_ok")
                staged = sem("staged")
                scattered = sem("scattered")
                step_s = sem("step")
                ND = 2 if first else 1
                ZC = 16
                ZERO = C // (2 * ZC)
                cleared = [*acc1, *acc2] if first else [*acc3, *acc4, *acc5, *acc6]
                zero = tmp("zero", [P, ZC * max(acc.shape[1] for acc in cleared)])
                zero_ok, zero_in = sem("zero_ok"), sem("zero_in")
                with nc.Block() as block:
                    @block.sync
                    def _(sp):
                        with sp.Fori(0, ITER) as i:
                            for b in range(2):
                                k = i * 2 + b
                                hold(sp, rows_free, k + 1)
                                sp.dma_start(rowd[:, b].rearrange("p s j -> p (s j)"),
                                             row_dst.rearrange("(k s) j -> k (s j)", s=B)[k].partition_broadcast(P)
                                             ).then_inc(rows_in[b], 16)
                                if first:
                                    sp.dma_start(rows_[:, b].rearrange("p s j -> p (s j)"),
                                                 row_src.rearrange("(k s) j -> k (s j)", s=B)[k].partition_broadcast(P)
                                                 ).then_inc(rows_in[b], 16)

                    @block.gpsimd
                    def _(pool):
                        g = nc.gpsimd

                        def gather(b, slots):
                            for s in slots:
                                pool.indirect_dma_start(ring[:, b, s, :], None, table,
                                                        bass.IndirectOffsetOnAxis(st_g[:, b, s:s + 1], 0)
                                                        ).then_inc(gat_in[b], 16)

                        pool.dma_start(primer, primed[:]).then_inc(scattered, 16)
                        for b in range(2):
                            g.tensor_copy(st_g[:, b], src_i[:, B * b:B * (b + 1)]).then_inc(staged, 1)
                        pool.wait_ge(staged, 2)
                        for b in range(2):
                            gather(b, range(B))
                        with pool.Fori(0, ITER) as i:
                            for b in range(2):
                                k = i * 2 + b
                                base = i * 6 + 3 * b + 2
                                hold(pool, scattered, (k * B + 1) * 16)
                                g.tensor_copy(st_d[:, b], dst_i[:, bass.ds(k * B, B)]).then_inc(staged, 1)
                                hold(pool, staged, base + 1)
                                for s in range(B):
                                    pool.indirect_dma_start(cur[:, b, s, :], None, replicas[s],
                                                            bass.IndirectOffsetOnAxis(st_d[:, b, s:s + 1], 0)
                                                            ).then_inc(cur_in[b], 16)
                                hold(pool, kept, k + 1)
                                hold(pool, masked_ok, k + 1)
                                g.tensor_copy(st_g[:, b], src_i[:, bass.ds(k * B + 2 * B, B)]).then_inc(staged, 1)
                                hold(pool, staged, base + 2)
                                gather(b, range(4))
                                hold(pool, new_ok, k + 1)
                                g.tensor_copy(st_u[:, b], uniq_dst[:, bass.ds(k * B, B)]).then_inc(staged, 1)
                                hold(pool, staged, base + 3)
                                for s in range(B):
                                    pool.indirect_dma_start(replicas[s],
                                                            bass.IndirectOffsetOnAxis(st_u[:, b, s:s + 1], 0),
                                                            new[:, b, s, :], None).then_inc(scattered, 16)
                                gather(b, range(4, B))
                        pool.wait_ge(scattered, (2 * ITER * B + 1) * 16)
                        for b in range(2):
                            pool.wait_ge(gat_in[b], (ITER + 1) * B * 16)

                    @block.scalar
                    def _(act):
                        def body(i, clearing):
                            for b in range(2):
                                k = i * 2 + b
                                for acc in cleared if clearing else []:
                                    w = acc.shape[1]
                                    act.dma_start(by_node(acc)[:, bass.ds(k * ZC, ZC), :],
                                                  zero[:, 0:ZC * w].rearrange("p (c w) -> p c w", w=w)
                                                  ).then_inc(zero_in, 16)
                                hold(act, gat_in[b], i * (B * 16) + B * 16)
                                nc.scalar.copy(keep[:, bass.ds(k * B, B), :], ring[:, b]).then_inc(kept, 1)

                        act.wait_ge(zero_ok, 1)
                        with act.Fori(0, ZERO) as i:
                            body(i, True)
                        with act.Fori(ZERO, ITER) as i:
                            body(i, False)
                        act.wait_ge(zero_in, 16 * 2 * ZERO * len(cleared))

                    @block.vector
                    def _(dve):
                        v = nc.vector
                        v.memset(zero[:], 0.0).then_inc(zero_ok, 1)
                        dve.sem_inc(rows_free, 2)
                        links = (2 + 2 + 3 if first else 2) + 1
                        with dve.Fori(0, ITER) as i:
                            step = Steps(dve, step_s, i * 2 * links)
                            for b in range(2):
                                k = i * 2 + b
                                cols = bass.ds(k * B, B)
                                v.tensor_copy(own[:, 1], src_f[:, cols])
                                step.link(v.tensor_copy(own[:, 0], dst_f[:, cols]))
                                hold(dve, rows_in[b], i * (16 * ND) + 16 * ND)
                                for s in range(B):
                                    last = v.tensor_scalar(pen[:, s], rowd[:, b, s], own[:, 0, s:s + 1], FAR,
                                                           ALU.not_equal, ALU.mult)
                                if first:
                                    step.link(last)
                                    for n, rr in enumerate((rowd, rows_)):
                                        for s in range(B):
                                            last = v.scalar_tensor_tensor(lone[:, s], rr[:, b, s], own[:, n, s:s + 1],
                                                                          earlier[:], ALU.is_equal, ALU.mult,
                                                                          accum_out=reps[:, n, s:s + 1])
                                        step.link(last)
                                    step.link(v.tensor_scalar(part[:], own[:], -1.0, spare[:], ALU.mult, ALU.add))
                                    step.link(v.scalar_tensor_tensor(part[:], reps[:], 0.0, part[:], ALU.is_gt, ALU.mult))
                                    v.tensor_tensor(uniq_dst[:, cols], part[:, 0], own[:, 0], ALU.add)
                                    step.link(v.tensor_tensor(uniq_src[:, cols], part[:, 1], own[:, 1], ALU.add))
                                else:
                                    step.link(last)
                                dve.sem_inc(rows_free, 1)
                                hold(dve, gat_in[b], i * (B * 16) + B * 16)
                                v.tensor_tensor(masked[:], bcast(pen[:].unsqueeze(2), [P, B, H, P]),
                                                bcast(ring[:, b, :, F:W].unsqueeze(3), [P, B, H, P]),
                                                ALU.add).then_inc(masked_ok, 1)
                                hold(dve, flipped, k + 1)
                                step.link(v.tensor_reduce(
                                    group[:], pv[:, :, 0:H * P].rearrange("p s (h j) -> p s h j", j=P), AX_X, ALU.max))
                                hold(dve, cur_in[b], i * (B * 16) + B * 16)
                                v.tensor_tensor(new[:, b], group[:], cur[:, b], ALU.max).then_inc(new_ok, 1)
                            assert step.n == 2 * links, step.n

                    @block.tensor
                    def _(pe):
                        with pe.Fori(0, ITER) as i:
                            for b in range(2):
                                hold(pe, masked_ok, i * 2 + b + 1)
                                for s in range(B):
                                    for h in range(H):
                                        last = nc.tensor.transpose(pv[:, s, h * P:(h + 1) * P], masked[:, s, h], ident[:])
                                last.then_inc(flipped, 1)

        def scatter_pass(tag, gathers, key, W, accs, messages, links, exp=None, expand=0, weights=None, extra=None):
            key_rows, key_f, key_u = key
            with ExitStack() as ctx:
                def tmp(name, shape, dt=F32):
                    return sb(f"{tag}_{name}", shape, dt, ctx)

                def sem(name):
                    return semaphore(ctx, f"{tag}_{name}")

                NG = len(gathers)
                NM = expand * P if expand else W
                keys = tmp("keys", [P, 2, B, P])
                same = tmp("same", [P, 2, B, P])
                own = tmp("own", [P, B])
                rings = [tmp(f"ring{n}", [P, 2, B, w]) for n, (_, _, w) in enumerate(gathers)]
                st_g = tmp("st_g", [P, 2, NG, B], I32)
                st_u = tmp("st_u", [P, 2, B], I32)
                msg = tmp("msg", [P, 2, B, NM])
                summed = tmp("summed", [P, expand, B, P]) if expand else None
                rows = tmp("rows", [P, 2, B, W])
                typs = tmp("typs", [P, 2, B, P]) if extra else None
                pick = tmp("pick", [P, B, P]) if extra else None
                ps = psum_all(ctx, f"{tag}_ps")
                ps_rows = [ps[:, 512 * b:512 * b + B * W].rearrange("p (s w) -> p s w", w=W) for b in range(2)]
                ps_mid = ps[:, 1024:1024 + 2048]
                keys_in = [sem("keys_in0"), sem("keys_in1")]
                gat_in = [sem("gat_in0"), sem("gat_in1")]
                same_ok = sem("same_ok")
                msg_ok = sem("msg_ok")
                pre_ok = sem("pre_ok")
                exp_ok = sem("exp_ok")
                pick_ok = sem("pick_ok")
                mats_ok = sem("mats_ok")
                sum_ok = sem("sum_ok")
                copy_ok = sem("copy_ok")
                prod_ok = sem("prod_ok")
                rows_ok = sem("rows_ok")
                rows_free = sem("rows_free")
                staged = sem("staged")
                scat = [sem("scat0"), sem("scat1")]
                step_s = sem("step")
                ND = 2 if extra else 1
                env = dict(rings=rings, msg=msg, pre_ok=pre_ok, exp_ok=exp_ok, pick_ok=pick_ok, mats_ok=mats_ok,
                           ps_mid=ps_mid, pick=pick, typs=typs)
                env["t"] = {}
                with nc.Block() as block:
                    @block.sync
                    def _(sp):
                        with sp.Fori(0, ITER) as i:
                            for b in range(2):
                                k = i * 2 + b
                                hold(sp, same_ok, k + 1)
                                sp.dma_start(keys[:, b].rearrange("p s j -> p (s j)"),
                                             key_rows.rearrange("(k s) j -> k (s j)", s=B)[k].partition_broadcast(P)
                                             ).then_inc(keys_in[b], 16)
                                if extra:
                                    hold(sp, pick_ok, k + 1)
                                    sp.dma_start(typs[:, b].rearrange("p s j -> p (s j)"),
                                                 row_typ.rearrange("(k s) j -> k (s j)", s=B)[k].partition_broadcast(P)
                                                 ).then_inc(keys_in[b], 16)

                    @block.gpsimd
                    def _(pool):
                        g = nc.gpsimd

                        def gather(b, s):
                            for n, (table, _, _) in enumerate(gathers):
                                pool.indirect_dma_start(rings[n][:, b, s, :], None, table,
                                                        bass.IndirectOffsetOnAxis(st_g[:, b, n, s:s + 1], 0)
                                                        ).then_inc(gat_in[b], 16)

                        pool.sem_inc(rows_free, 1)
                        for r in range(2):
                            pool.dma_start(primer, primed[:]).then_inc(scat[r], 16)
                            pool.wait_ge(scat[r], 16)
                        for b in range(2):
                            for n, (_, idx, _) in enumerate(gathers):
                                g.tensor_copy(st_g[:, b, n], idx[:, B * b:B * (b + 1)]).then_inc(staged, 1)
                        pool.wait_ge(staged, 2 * NG)
                        for b in range(2):
                            for s in range(B):
                                gather(b, s)
                        with pool.Fori(0, ITER) as i:
                            count = [0, 0]
                            for b in range(2):
                                k = i * 2 + b
                                hold(pool, msg_ok, k + 1)
                                for n, (_, idx, _) in enumerate(gathers):
                                    g.tensor_copy(st_g[:, b, n], idx[:, bass.ds(k * B + 2 * B, B)]).then_inc(staged, 1)
                                g.tensor_copy(st_u[:, b], key_u[:, bass.ds(k * B, B)]).then_inc(staged, 1)
                                hold(pool, staged, (i * 2 + b + 1) * (NG + 1) + 2 * NG)
                                for s in range(2):
                                    gather(b, s)
                                hold(pool, rows_ok, k + 3)
                                for s in range(B):
                                    r = (s + b) % 2
                                    hold(pool, scat[r], (i * B + count[r] + 1) * 16)
                                    pool.indirect_dma_start(accs[r], bass.IndirectOffsetOnAxis(st_u[:, b, s:s + 1], 0),
                                                            rows[:, b, s, :], None, compute_op=ALU.add
                                                            ).then_inc(scat[r], 16)
                                    count[r] += 1
                                    if s + 2 < B:
                                        gather(b, s + 2)
                                    if s == 1:
                                        pool.sem_inc(rows_free, 1)
                        for r in range(2):
                            pool.wait_ge(scat[r], (ITER * B + 1) * 16)
                        for b in range(2):
                            pool.wait_ge(gat_in[b], (ITER + 1) * B * NG * 16)

                    @block.vector
                    def _(dve):
                        v = nc.vector
                        dve.sem_inc(same_ok, 2)
                        if extra:
                            dve.sem_inc(pick_ok, 2)
                        with dve.Fori(0, ITER) as i:
                            step = Steps(dve, step_s, i * (2 * (links + 1)))
                            for b in range(2):
                                k = i * 2 + b
                                step.link(v.tensor_copy(own[:], key_f[:, bass.ds(k * B, B)]))
                                hold(dve, keys_in[b], i * (16 * ND) + 16 * ND)
                                hold(dve, prod_ok, k + 1)
                                v.tensor_tensor(same[:, b], keys[:, b], bcast(own[:].unsqueeze(2), [P, B, P]),
                                                ALU.is_equal).then_inc(same_ok, 1)
                                gathered = (gat_in[b], i * (B * NG * 16) + B * NG * 16)
                                messages(dve, step, env, k, b, gathered).then_inc(msg_ok, 1)
                            assert step.n == 2 * (links + 1), step.n

                    @block.tensor
                    def _(pe):
                        mm = nc.tensor.matmul
                        pe.sem_inc(prod_ok, 2)
                        with pe.Fori(0, ITER) as i:
                            for b in range(2):
                                k = i * 2 + b
                                if extra:
                                    hold(pe, pick_ok, k + 3)
                                    for s in range(B):
                                        last = mm(ps_mid[:, 256 * s:256 * (s + 1)], pick[:, s],
                                                  w_rel[:].rearrange("p i o -> p (i o)"), start=True, stop=True)
                                    last.then_inc(mats_ok, 1)
                                hold(pe, msg_ok, k + 1)
                                if expand:
                                    hold(pe, copy_ok, k + 1)
                                    for a in range(expand):
                                        for s in range(B):
                                            last = mm(ps_mid[:, 1024 * a + P * s:1024 * a + P * (s + 1)],
                                                      msg[:, b, s, P * a:P * (a + 1)], same[:, b, s],
                                                      start=True, stop=True)
                                    last.then_inc(sum_ok, 1)
                                    hold(pe, copy_ok, k + 2)
                                hold(pe, rows_ok, k + 1)
                                for s in range(B):
                                    if expand:
                                        for a in range(expand):
                                            last = mm(ps_rows[b][:, s], summed[:, a, s], weights(a),
                                                      start=(a == 0), stop=(a == expand - 1))
                                    else:
                                        last = mm(ps_rows[b][:, s], same[:, b, s], msg[:, b, s], start=True, stop=True)
                                last.then_inc(prod_ok, 1)

                    @block.scalar
                    def _(act):
                        act.sem_inc(rows_ok, 2)
                        if expand:
                            act.sem_inc(copy_ok, 1)
                        with act.Fori(0, ITER) as i:
                            for b in range(2):
                                k = i * 2 + b
                                if exp:
                                    hold(act, pre_ok, k + 1)
                                    exp(env, b).then_inc(exp_ok, 1)
                                if expand:
                                    hold(act, sum_ok, k + 1)
                                    for a in range(expand):
                                        last = nc.scalar.copy(summed[:, a].rearrange("p s j -> p (s j)"),
                                                              ps_mid[:, 1024 * a:1024 * a + B * P])
                                    last.then_inc(copy_ok, 1)
                                hold(act, prod_ok, k + 3)
                                hold(act, rows_free, k + 1)
                                nc.scalar.copy(rows[:, b], ps_rows[b]).then_inc(rows_ok, 1)

        key_dst = (row_dst, dst_f, uniq_dst)
        key_src = (row_src, src_f, uniq_src)

        kept1 = ExitStack()
        keep1 = sb("keep1", [P, T, FEAT + HEADS1], F32, kept1)
        segment_max("m1", t_gat1, max1, HEADS1, FEAT, keep1, True)

        def settle_max(tag, replicas, H, as_, ad_, self_, table, counts):
            PIECES = 2
            CP = C // PIECES
            with ExitStack() as ctx:
                def sem(name):
                    return semaphore(ctx, f"{tag}_{name}")

                W = 2 * H + (NREL if counts is not None else 0)
                two = sb(f"{tag}_two", [P, 2, C, H], F32, ctx)
                m = sb(f"{tag}_m", [P, C, H], F32, ctx)
                e = self_
                row = sb(f"{tag}_row", [P, CP, W], F32, ctx)
                in_ = [sem("in0"), sem("in1")]
                step_s, row_ok, arg_ok, out_s = sem("step"), sem("row_ok"), sem("arg_ok"), sem("out")
                with nc.Block() as block:
                    @block.sync
                    def _(sp):
                        for n, rep in enumerate(replicas):
                            if n >= 2:
                                sp.wait_ge(step_s, n - 1)
                            sp.dma_start(two[:, n % 2], by_node(rep)).then_inc(in_[n % 2], 16)
                        for piece in range(PIECES):
                            sp.wait_ge(row_ok, piece + 1)
                            sp.dma_start(by_node(table)[:, piece * CP:(piece + 1) * CP, :], row[:]
                                         ).then_inc(out_s, 16)
                        sp.wait_ge(out_s, 16 * PIECES)

                    @block.vector
                    def _(dve):
                        v = nc.vector
                        step = Steps(dve, step_s)
                        for n in range(B):
                            dve.wait_ge(in_[n % 2], 16 * (n // 2 + 1))
                            step.link(v.tensor_copy(m[:], two[:, 0]) if n == 0 else
                                      v.tensor_tensor(m[:], m[:], two[:, n % 2], ALU.max))
                        step.link(v.tensor_tensor(m[:], m[:], ad_[:], ALU.add))
                        step.link(v.scalar_tensor_tensor(m[:], m[:], SLOPE, m[:], ALU.mult, ALU.max))
                        for piece in range(PIECES):
                            cols = slice(piece * CP, (piece + 1) * CP)
                            if piece:
                                dve.wait_ge(out_s, 16 * piece)
                            v.tensor_copy(row[:, :, 0:H], m[:, cols, :])
                            if counts is not None:
                                v.tensor_copy(row[:, :, 2 * H:W], counts[:, cols, :])
                            v.tensor_copy(row[:, :, H:2 * H], ad_[:, cols, :]).then_inc(row_ok, 1)
                        step.link(v.tensor_tensor(e[:], as_[:], ad_[:], ALU.add))
                        step.link(v.scalar_tensor_tensor(e[:], e[:], SLOPE, e[:], ALU.mult, ALU.max))
                        v.tensor_tensor(e[:], e[:], m[:], ALU.subtract).then_inc(arg_ok, 1)

                    @block.scalar
                    def _(act):
                        act.wait_ge(arg_ok, 1)
                        nc.scalar.activation(self_[:], e[:], ACT.Exp)

        settle_max("s1", max1, HEADS1, as1, ad1, self1, t_norm1, None)

        with ExitStack() as ctx:
            arg = sb("arg1", [P, B, HEADS1], F32, ctx)
            wgt = sb("wgt1", [P, B, HEADS1], F32, ctx)
            rel = sb("rel1", [P, B], F32, ctx)

            def gat1_messages(dve, step, env, k, b, gathered):
                v = nc.vector
                cols = bass.ds(k * B, B)
                norm, msg = env["rings"][0], env["msg"]
                hold(dve, *gathered)
                v.tensor_copy(rel[:], rel_f[:, cols])
                step.link(v.tensor_tensor(arg[:], keep1[:, cols, FEAT:FEAT + HEADS1], norm[:, b, :, HEADS1:2 * HEADS1],
                                          ALU.add))
                step.link(v.scalar_tensor_tensor(arg[:], arg[:], SLOPE, arg[:], ALU.mult, ALU.max))
                v.tensor_tensor(arg[:], arg[:], norm[:, b, :, 0:HEADS1], ALU.subtract).then_inc(env["pre_ok"], 1)
                v.tensor_tensor(msg[:, b, :, WIDTH1 - NREL:WIDTH1], bcast(rel[:].unsqueeze(2), [P, B, NREL]),
                                bcast(iota8[:].unsqueeze(1), [P, B, NREL]), ALU.is_equal)
                hold(dve, env["exp_ok"], k + 1)
                v.tensor_copy(msg[:, b, :, HEADS1 * FEAT:HEADS1 * FEAT + HEADS1], wgt[:])
                return v.tensor_tensor(
                    msg[:, b, :, 0:HEADS1 * FEAT].rearrange("p s (h f) -> p s h f", f=FEAT),
                    bcast(keep1[:, cols, 0:FEAT].unsqueeze(2), [P, B, HEADS1, FEAT]),
                    bcast(wgt[:].unsqueeze(3), [P, B, HEADS1, FEAT]), ALU.mult)

            scatter_pass("g1", [(t_norm1, dst_i, 2 * HEADS1)], key_dst, WIDTH1, acc1, gat1_messages, 2,
                         exp=lambda env, b: nc.scalar.activation(wgt[:], arg[:], ACT.Exp))
        kept1.close()

        def stream(sp, half, Q, loads, in_, read, store, row_ok, out_s):
            def load(k, b):
                for to, frm in loads:
                    sp.dma_start(to[:, b], by_node(frm)[:, bass.ds(k * Q, Q), :]).then_inc(in_[b], 16)

            def put(k, b):
                hold(sp, row_ok, k + 3)
                sp.dma_start(*store(k, b)).then_inc(out_s[b], 16)

            def load_third(k, b):
                for sem in read:
                    hold(sp, sem, k + 2)
                load(k + 3, 1 - b)

            for b in range(2):
                sp.dma_start(primer, primed[:]).then_inc(out_s[b], 16)
                sp.wait_ge(out_s[b], 16)
            load(0, 0)
            load(1, 1)
            load_third(-1, 1)
            with sp.Fori(0, half - 2) as i:
                for b in range(2):
                    load_third(i * 2 + b, b)
                    put(i * 2 + b, b)
            load_third(2 * half - 4, 0)
            for k in range(2 * half - 4, 2 * half):
                put(k, k % 2)
            for b in range(2):
                sp.wait_ge(out_s[b], 16 * (half + 1))

        with ExitStack() as ctx:
            def tmp(name, shape, dt=F32):
                return sb(f"d2_{name}", shape, dt, ctx)

            def sem(name):
                return semaphore(ctx, f"d2_{name}")

            Q = 16
            PAIRS = Q // 2
            HALF = C // Q // 2
            HF = HEADS1 * FEAT
            a0, a1 = tmp("a0", [P, 2, Q, WIDTH1]), tmp("a1", [P, 2, Q, WIDTH1])
            hs = tmp("hs", [P, 2, Q, FEAT + HEADS1])
            agg = tmp("agg", [P, Q, WIDTH1])
            mix = tmp("mix", [P, 2, Q, HF])
            z = tmp("z", [P, 2, Q, HEADS1])
            mix_t = tmp("mix_t", [HID, PAIRS * P])
            pos = tmp("pos", [HID, 4, 512])
            ex = tmp("ex", [HID, 4, 512])
            act_t = tmp("act_t", [HID, 4, 512])
            row = tmp("row", [P, 2, Q, CH + 1])
            ps = psum_all(ctx, "d2_ps")
            ps_o = ps[:, 3072:4096].rearrange("p (a z) -> p a z", z=512)[:, :, 0:8 * (CH + 2)].rearrange(
                "p a (n w) -> p a n w", w=CH + 2)
            in_ = [sem("in0"), sem("in1")]
            out_s = [sem("out0"), sem("out1")]
            step_s, pstep_s = sem("step"), sem("pstep")
            sum_ok = sem("sum_ok")
            mix_ok = sem("mix_ok")
            flip_ok, up_ok, down_ok = sem("flip_ok"), sem("up_ok"), sem("down_ok")
            copy_ok, exp_ok = sem("copy_ok"), sem("exp_ok")
            act_ok, row_ok = sem("act_ok"), sem("row_ok")
            m_s = sem("m_s")
            with nc.Block() as block:
                @block.sync
                def _(sp):
                    stream(sp, HALF, Q, [(a0, acc1[0]), (a1, acc1[1]), (hs, t_gat1)], in_, [sum_ok],
                           lambda k, b: (by_node(t_gat2)[:, bass.ds(k * Q, Q), :], row[:, b]), row_ok, out_s)
                    for table in max2:
                        sp.dma_start(by_node(table), as2[:]).then_inc(m_s, 16)
                    sp.wait_ge(m_s, 16 * B)

                @block.gpsimd
                def _(pool):
                    g = nc.gpsimd
                    with pool.Fori(0, HALF) as i:
                        step = Steps(pool, pstep_s, i * 10, apart=True)
                        for b in range(2):
                            k = i * 2 + b
                            cols = bass.ds(k * Q, Q)
                            hold(pool, in_[b], i * 48 + 48)
                            hold(pool, flip_ok, k + 1)
                            step.link(g.tensor_tensor(agg[:], a0[:, b], a1[:, b], ALU.add))
                            step.link(g.tensor_tensor(z[:, b], agg[:, :, HF:HF + HEADS1], self1[:, cols, :], ALU.add))
                            step.link(g.tensor_copy(counts[:, cols, :], agg[:, :, WIDTH1 - NREL:WIDTH1]))
                            step.link(g.tensor_tensor(
                                mix[:, b].rearrange("p q (h f) -> p q h f", f=FEAT),
                                bcast(hs[:, b, :, 0:FEAT].unsqueeze(2), [P, Q, HEADS1, FEAT]),
                                bcast(self1[:, cols, :].unsqueeze(3), [P, Q, HEADS1, FEAT]), ALU.mult))
                            step.link(g.tensor_tensor(mix[:, b], mix[:, b], agg[:, :, 0:HF], ALU.add))
                            pool.sem_inc(sum_ok, 1)

                @block.tensor
                def _(pe):
                    mm = nc.tensor.matmul
                    pe.sem_inc(flip_ok, 2)

                    def flip(i, b):
                        hold(pe, mix_ok, i * 2 + b + 1)
                        for n in range(PAIRS):
                            last = nc.tensor.transpose(ps[0:HID, P * n:P * (n + 1)],
                                                       mix[:, b, 2 * n:2 * n + 2, :].rearrange("p a f -> p (a f)"),
                                                       ident[:])
                        last.then_inc(flip_ok, 1)

                    def body(i, b, following, _):
                        k = i * 2 + b
                        hold(pe, copy_ok, k + 1)
                        hold(pe, exp_ok, k * 4 + 4)
                        for u in range(4):
                            j, q = u // 2, u % 2
                            mm(ps[0:HID, 1024 + 512 * u:1536 + 512 * u],
                               w1_half[:, j].rearrange("p h c -> p (h c)"), mix_t[:, 512 * q:512 * (q + 1)],
                               start=True, stop=True).then_inc(up_ok, 1)
                        if following:
                            flip(*following)
                        hold(pe, row_ok, k + 2)
                        for u in range(4):
                            j, q = u // 2, u % 2
                            hold(pe, act_ok, k * 4 + u + 1)
                            for n in range(4):
                                node = 2 * (4 * q + n) + j
                                last = mm(ps_o[:, node // 8, node % 8], act_t[:, u, P * n:P * (n + 1)], w2_ext[:],
                                          start=True, stop=True)
                        last.then_inc(down_ok, 1)

                    flip(0, 0)
                    each_chunk(pe, HALF, body)

                @block.scalar
                def _(act):
                    act.sem_inc(exp_ok, 4)

                    def copy(i, b):
                        hold(act, flip_ok, i * 2 + b + 3)
                        nc.scalar.copy(mix_t[:], ps[0:HID, 0:PAIRS * P]).then_inc(copy_ok, 1)

                    def body(i, b, following, _):
                        k = i * 2 + b
                        for u in range(4):
                            hold(act, up_ok, k * 4 + u + 1)
                            view = ps[0:HID, 1024 + 512 * u:1536 + 512 * u]
                            nc.scalar.activation(pos[:, u], view, ACT.Relu, bias=b1_col[:, 1:2],
                                                 scale=1.0 / SELU_ALPHA)
                            nc.scalar.activation(ex[:, u], view, ACT.Exp, bias=b1_col[:, 0:1]).then_inc(exp_ok, 1)
                        if following:
                            copy(*following)

                    copy(0, 0)
                    each_chunk(act, HALF, body)

                @block.vector
                def _(dve):
                    v = nc.vector
                    dve.sem_inc(row_ok, 2)
                    half = lambda ap: ap.rearrange("p (a n) w -> p a n w", n=8)

                    def normalise(i, b):
                        k = i * 2 + b
                        step = Steps(dve, step_s, k * 2)
                        heads = mix[:, b].rearrange("p q (h f) -> p q h f", f=FEAT)
                        hold(dve, sum_ok, k + 1)
                        step.link(v.tensor_scalar(z[:, b], z[:, b], 1e-16, None, ALU.add))
                        step.link(v.reciprocal(z[:, b], z[:, b]))
                        v.tensor_tensor(heads, heads, bcast(z[:, b].unsqueeze(3), [P, Q, HEADS1, FEAT]), ALU.mult
                                        ).then_inc(mix_ok, 1)

                    def body(i, b, following, _):
                        k = i * 2 + b
                        if following:
                            normalise(*following)
                        for u in range(4):
                            hold(dve, exp_ok, k * 4 + u + 5)
                            v.scalar_tensor_tensor(act_t[:, u], ex[:, u], 1.0, pos[:, u], ALU.min, ALU.add
                                                   ).then_inc(act_ok, 1)
                        hold(dve, down_ok, k + 1)
                        hold(dve, out_s[b], i * 16 + 16)
                        const = bcast(w2_const[:].unsqueeze(1).unsqueeze(1), [P, 2, 8, CH + 2])
                        for to, lo, hi in ((as2[:, bass.ds(k * Q, Q), :], CH, CH + 1),
                                           (ad2[:, bass.ds(k * Q, Q), :], CH + 1, CH + 2),
                                           (row[:, b], 0, CH + 1)):
                            last = v.tensor_tensor(half(to), ps_o[:, :, :, lo:hi], const[:, :, :, lo:hi], ALU.add)
                        last.then_inc(row_ok, 1)

                    normalise(0, 0)
                    each_chunk(dve, HALF, body)
        gat.close()

        kept2 = ExitStack()
        keep2 = sb("keep2", [P, T, CH + 1], F32, kept2)
        segment_max("m2", t_gat2, max2, 1, CH, keep2, False)
        settle_max("s2", max2, 1, as2, ad2, self2, t_norm2, counts)

        with ExitStack() as ctx:
            arg = sb("arg2", [P, B, 1], F32, ctx)
            wgt = sb("wgt2", [P, B, 1], F32, ctx)
            rel = sb("rel2", [P, B], F32, ctx)
            hot = sb("hot2", [P, B, NREL], F32, ctx)
            cnt = sb("cnt2", [P, B], F32, ctx)

            def gat2_messages(dve, step, env, k, b, gathered):
                v = nc.vector
                cols = bass.ds(k * B, B)
                norm, msg = env["rings"][0], env["msg"]
                hold(dve, *gathered)
                step.link(v.tensor_copy(rel[:], rel_f[:, cols]))
                step.link(v.tensor_tensor(arg[:], keep2[:, cols, CH:CH + 1], norm[:, b, :, 1:2], ALU.add))
                step.link(v.scalar_tensor_tensor(arg[:], arg[:], SLOPE, arg[:], ALU.mult, ALU.max))
                v.tensor_tensor(arg[:], arg[:], norm[:, b, :, 0:1], ALU.subtract).then_inc(env["pre_ok"], 1)
                step.link(v.tensor_tensor(hot[:], bcast(rel[:].unsqueeze(2), [P, B, NREL]),
                                          bcast(iota8[:].unsqueeze(1), [P, B, NREL]), ALU.is_equal))
                step.link(v.tensor_tensor(hot[:], hot[:], norm[:, b, :, 2:2 + NREL], ALU.mult))
                step.link(v.tensor_reduce(cnt[:], hot[:], AX_X, ALU.add))
                step.link(v.tensor_scalar(cnt[:], cnt[:], 1.0, None, ALU.max))
                v.reciprocal(inv_cnt[:, cols], cnt[:])
                hold(dve, env["exp_ok"], k + 1)
                v.tensor_copy(msg[:, b, :, CH:CH + 1], wgt[:])
                return v.tensor_tensor(msg[:, b, :, 0:CH], keep2[:, cols, 0:CH], bcast(wgt[:], [P, B, CH]), ALU.mult)

            scatter_pass("g2", [(t_norm2, dst_i, 2 + NREL)], key_dst, WIDTH2, acc2, gat2_messages, 7,
                         exp=lambda env, b: nc.scalar.activation(wgt[:], arg[:], ACT.Exp))
        kept2.close()

        QN = 40
        WIDE = 80

        def node_pass(tag, loads, table, width_out, alloc, prepare, prep_links, parts, part_links, flips=None, wide=0,
                      bd=None, act_mid=None, norm=True, store=None, QN=QN, read=("prep_ok",)):
            early, middle, ready, end = parts
            e_links, m_links, r_links, l_links = part_links
            with ExitStack() as ctx:
                def tmp(name, shape, dt=F32):
                    return sb(f"{tag}_{name}", shape, dt, ctx)

                def sem(name):
                    return semaphore(ctx, f"{tag}_{name}")

                HN = C // QN // 2
                ins = [(tmp(f"in{n}", [P, 2, QN, t.shape[1]]), t) for n, t in enumerate(loads)]
                row = tmp("row", [P, 2, QN, width_out]) if table is not None else None
                t = ln_buffers(ctx, QN, tag) if norm else None
                ps = psum_all(ctx, f"{tag}_ps")
                in_ = [sem("in0"), sem("in1")]
                out_s = [sem("out0"), sem("out1")]
                names = ("step", "pstep", "prep_ok", "mid_ok", "exp_ok", "flip_in", "flip_ok", "copy_ok",
                         "prod_ok", "used_ok", "row_ok", "early_ok")
                env = {n: sem(n) for n in names}
                cols_in = QN * (flips or 0)
                n_flip = cols_in // P
                cols_out = n_flip * wide
                assert cols_in <= 1280 and cols_out <= 1280
                at = [1536, 2560] if cols_out <= 1024 else [1024, 2560]
                assert not flips or cols_in <= at[0]
                env.update(ins=[a for a, _ in ins], row=row, t=t, width=QN,
                           ps_out=[ps[:, at[b]:at[b] + cols_out] for b in range(2)] if flips else None)
                env["flip_src"] = lambda b: ins[-1][0][:, b].rearrange("p q f -> p (q f)")
                env.update(alloc(tmp))
                flipped = tmp("flipped", [P, cols_in]) if flips else None

                with nc.Block() as block:
                    @block.sync
                    def _(sp):
                        stream(sp, HN, QN, ins, in_,
                               [env[n] for n in read],
                               store or (lambda k, b: (by_node(table)[:, bass.ds(k * QN, QN), :], row[:, b])),
                               env["row_ok"], out_s)

                    @block.gpsimd
                    def _(pool):
                        with pool.Fori(0, HN) as i:
                            step = Steps(pool, env["pstep"], i * 2 * prep_links, apart=True)
                            for b in range(2):
                                k = i * 2 + b
                                hold(pool, in_[b], i * (16 * len(loads)) + 16 * len(loads))
                                hold(pool, env["exp_ok" if act_mid else "used_ok"], k + 1)
                                prepare(env, step, k, b)
                                pool.sem_inc(env["prep_ok"], 1)
                            assert step.n == 2 * prep_links, step.n

                    @block.vector
                    def _(dve):
                        dve.sem_inc(env["row_ok"], 2)
                        dve.sem_inc(env["used_ok"], 2)
                        ahead = e_links + r_links
                        total = ahead + m_links + l_links

                        def first_half(i, b, step):
                            k = i * 2 + b
                            hold(dve, env["prep_ok"], k + 1)
                            early(dve, env, step, k, b)
                            if "early_ok" in read:
                                dve.sem_inc(env["early_ok"], 1)

                        def body(i, b, following, second):
                            k = i * 2 + b
                            step = Steps(dve, env["step"], ahead + (e_links if act_mid else 0) + k * total)
                            if not following and act_mid:
                                step.base -= e_links
                            middle(dve, env, step, k, b)
                            if following:
                                if not act_mid:
                                    first_half(*following, step)
                                ready(dve, env, step, following[0] * 2 + following[1], following[1])
                            front(dve, env, step, k)
                            if second and act_mid:
                                first_half(*second, step)
                            if table is not None:
                                hold(dve, out_s[b], i * 16 + 16)
                            end(dve, env, step, k, b)
                            made = m_links + l_links + (r_links if following else 0)
                            made += e_links if (second if act_mid else following) else 0
                            assert step.n == made, step.n

                        step = Steps(dve, env["step"])
                        first_half(0, 0, step)
                        ready(dve, env, step, 0, 0)
                        if act_mid:
                            first_half(0, 1, step)
                        each_chunk(dve, HN, body)

                    if flips:
                        @block.tensor
                        def _(pe):
                            with pe.Fori(0, HN) as i:
                                for b in range(2):
                                    k = i * 2 + b
                                    if act_mid:
                                        hold(pe, env["flip_in"], k + 1)
                                    else:
                                        hold(pe, in_[b], i * (16 * len(loads)) + 16 * len(loads))
                                    for n in range(n_flip):
                                        last = nc.tensor.transpose(ps[:, P * n:P * (n + 1)],
                                                                   env["flip_src"](b)[:, P * n:P * (n + 1)], ident[:])
                                    last.then_inc(env["flip_ok"], 1)
                                    hold(pe, env["copy_ok"], k + 1)
                                    hold(pe, env["used_ok"], k + 1)
                                    for n in range(n_flip):
                                        last = nc.tensor.matmul(env["ps_out"][b][:, wide * n:wide * (n + 1)],
                                                                flipped[:, P * n:P * (n + 1)], bd, start=True, stop=True)
                                    last.then_inc(env["prod_ok"], 1)

                    if flips or norm:
                        @block.scalar
                        def _(act):
                            def exp(i, b):
                                if act_mid:
                                    hold(act, env["mid_ok"], i * 2 + b + 1)
                                    act_mid(env, b).then_inc(env["exp_ok"], 1)

                            def copy(i, b):
                                if flips:
                                    hold(act, env["flip_ok"], i * 2 + b + 1)
                                    nc.scalar.copy(flipped[:], ps[:, 0:cols_in]).then_inc(env["copy_ok"], 1)

                            def body(i, b, following, second):
                                if following:
                                    copy(*following)
                                if norm:
                                    take_root(act, t, i * 2 + b)
                                if second:
                                    exp(*second)

                            if act_mid:
                                act.sem_inc(env["exp_ok"], 2)
                            exp(0, 0)
                            copy(0, 0)
                            exp(0, 1)
                            each_chunk(act, HN, body)

        def none(dve, env, step, k, b):
            pass

        def front(dve, env, step, k):
            if env["t"]:
                ln_front(step, X[:, bass.ds(k * env["width"], env["width"]), :], env["t"], k)

        def columns(ap, w):
            return ap.rearrange("p (q w) -> p q w", w=w)

        def d4_alloc(tmp):
            ex = tmp("ex", [P, 2, QN, CH])
            return dict(agg=tmp("agg", [P, QN, WIDTH2]), mix=tmp("mix", [P, 2, QN, CH]), z=tmp("z", [P, 2, QN, 1]),
                        pos=tmp("pos", [P, QN, CH]), ex=ex,
                        flip_src=lambda b: ex[:, b].rearrange("p q f -> p (q f)"))

        def d4_prepare(env, step, k, b):
            g = nc.gpsimd
            a0, a1, hs = env["ins"]
            agg, mix, z = env["agg"], env["mix"][:, b], env["z"][:, b]
            cols = bass.ds(k * QN, QN)
            step.link(g.tensor_tensor(agg[:], a0[:, b], a1[:, b], ALU.add))
            step.link(g.tensor_tensor(z, agg[:, :, CH:CH + 1], self2[:, cols, :], ALU.add))
            step.link(g.tensor_tensor(mix, hs[:, b, :, 0:CH], bcast(self2[:, cols, :], [P, QN, CH]), ALU.mult))
            step.link(g.tensor_tensor(mix, mix, agg[:, :, 0:CH], ALU.add))

        def d4_early(dve, env, step, k, b):
            v = nc.vector
            mix, z = env["mix"][:, b], env["z"][:, b]
            step.link(v.tensor_scalar(z, z, 1e-16, None, ALU.add))
            step.link(v.reciprocal(z, z))
            step.link(v.tensor_tensor(mix, mix, bcast(z, [P, QN, CH]), ALU.mult))
            v.tensor_tensor(mix, mix, bcast(b2_row[:].unsqueeze(1), [P, QN, CH]), ALU.add).then_inc(env["mid_ok"], 1)

        def d4_exp(env, b):
            nc.scalar.activation(env["pos"][:], env["mix"][:, b], ACT.Relu, scale=1.0 / SELU_ALPHA)
            return nc.scalar.activation(env["ex"][:, b], env["mix"][:, b], ACT.Exp)

        def d4_ready(dve, env, step, k, b):
            hold(dve, env["exp_ok"], k + 3)
            ex = env["ex"][:, b]
            nc.vector.scalar_tensor_tensor(ex, ex, 1.0, env["pos"][:], ALU.min, ALU.add).then_inc(env["flip_in"], 1)

        def d4_middle(dve, env, step, k, b):
            v = nc.vector
            xc = X[:, bass.ds(k * QN, QN), :]
            step.link(v.tensor_tensor(xc, xc, bcast(wf_const[:].unsqueeze(1), [P, QN, FEAT]), ALU.add))
            hold(dve, env["prod_ok"], k + 1)
            step.link(v.tensor_tensor(xc, xc, columns(env["ps_out"][b], FEAT), ALU.add))
            dve.sem_inc(env["used_ok"], 1)

        def norm_end(dve, env, step, k, b):
            ln_back(dve, step, env["row"][:, b], env["t"], k).then_inc(env["row_ok"], 1)

        node_pass("d4", [acc2[0], acc2[1], t_gat2], t_rel1, FEAT, d4_alloc, d4_prepare, 4,
                  (d4_early, d4_middle, d4_ready, norm_end), (3, 2 + LN_FRONT, 0, LN_BACK),
                  flips=CH, wide=4 * FEAT, bd=bd_wf[:].rearrange("p j c -> p (j c)"), act_mid=d4_exp)
        counts_ctx.close()

        def relation_messages(tag, F, ctx):
            rel = sb(f"{tag}_rel", [P, B], F32, ctx)
            inv = sb(f"{tag}_inv", [P, B], F32, ctx)
            hot = sb(f"{tag}_hot", [P, B, NREL], F32, ctx)

            def messages(dve, step, env, k, b, gathered):
                v = nc.vector
                cols = bass.ds(k * B, B)
                v.tensor_copy(inv[:], inv_cnt[:, cols])
                step.link(v.tensor_copy(rel[:], rel_f[:, cols]))
                step.link(v.tensor_tensor(hot[:], bcast(rel[:].unsqueeze(2), [P, B, NREL]),
                                          bcast(iota8[:].unsqueeze(1), [P, B, NREL]), ALU.is_equal))
                step.link(v.tensor_tensor(hot[:], hot[:], bcast(inv[:].unsqueeze(2), [P, B, NREL]), ALU.mult))
                hold(dve, *gathered)
                for s in range(B):
                    last = v.tensor_tensor(env["msg"][:, b, s].rearrange("p (r f) -> p r f", f=F),
                                           bcast(env["rings"][0][:, b, s].unsqueeze(1), [P, NREL, F]),
                                           bcast(hot[:, s].unsqueeze(2), [P, NREL, F]), ALU.mult)
                return last
            return messages

        with ExitStack() as ctx:
            scatter_pass("r1", [(t_rel1, src_i, FEAT)], key_dst, CH, acc3, relation_messages("r1m", FEAT, ctx), 3,
                         expand=1, weights=lambda a: rel_w1[:])

        def sum_alloc(W):
            def alloc(tmp):
                agg = tmp("agg", [P, 2, QN, W])
                return dict(agg=agg)
            return alloc

        def sum_prepare(bias, W):
            def prepare(env, step, k, b):
                g, agg = nc.gpsimd, env["agg"][:, b]
                a0, a1 = env["ins"][0:2]
                step.link(g.tensor_tensor(agg, a0[:, b], a1[:, b], ALU.add))
                step.link(g.tensor_tensor(agg, agg, bcast(bias[:].unsqueeze(1), [P, QN, W]), ALU.add))
            return prepare

        def d5_middle(dve, env, step, k, b):
            agg = env["agg"][:, b]
            hold(dve, env["prod_ok"], k + 1)
            step.link(nc.vector.tensor_tensor(agg, agg, columns(env["ps_out"][b], CH), ALU.add))

        def d5_end(dve, env, step, k, b):
            step.link(nc.vector.tensor_scalar(env["row"][:, b], env["agg"][:, b], 0.0, None, ALU.max))
            dve.sem_inc(env["used_ok"], 1)
            dve.sem_inc(env["row_ok"], 1)

        node_pass("d5", [acc3[0], acc3[1], t_rel1], t_rel2, CH, sum_alloc(CH), sum_prepare(rb1_row, CH), 2,
                  (none, d5_middle, none, d5_end), (0, 1, 0, 1), flips=FEAT, wide=8 * CH,
                  bd=bd_root1[:].rearrange("p j c -> p (j c)"), norm=False, read=("prep_ok", "flip_ok"))

        with ExitStack() as ctx:
            scatter_pass("r2", [(t_rel2, src_i, CH)], key_dst, FEAT, acc4, relation_messages("r2m", CH, ctx), 3,
                         expand=2, weights=lambda a: rel_w2[:, a])

        def d6_middle(dve, env, step, k, b):
            v = nc.vector
            xc = X[:, bass.ds(k * QN, QN), :]
            step.link(v.tensor_tensor(xc, xc, env["agg"][:, b], ALU.add))
            hold(dve, env["prod_ok"], k + 1)
            step.link(v.tensor_tensor(xc, xc, columns(env["ps_out"][b], FEAT), ALU.add))
            dve.sem_inc(env["used_ok"], 1)

        node_pass("d6", [acc4[0], acc4[1], t_rel2], t_mix, FEAT, sum_alloc(FEAT), sum_prepare(rb2_row, FEAT), 2,
                  (none, d6_middle, none, norm_end), (0, 2 + LN_FRONT, 0, LN_BACK), flips=CH, wide=4 * FEAT,
                  bd=bd_root2[:].rearrange("p j c -> p (j c)"), read=("prep_ok", "flip_ok"))

        D_, E_, H_ = 5.0, 0.9, 0.1
        with ExitStack() as ctx:
            wts = sb("l2_wts", [P, B], F32, ctx)
            den = sb("l2_den", [P, B, FEAT], F32, ctx)
            num = sb("l2_num", [P, B, FEAT], F32, ctx)

            def l2_messages(dve, step, env, k, b, gathered):
                v = nc.vector
                xi, xj = (r[:, b] for r in env["rings"])
                v.tensor_copy(wts[:], weight[:, bass.ds(k * B, B)])
                hold(dve, *gathered)
                step.link(v.tensor_scalar(den[:], xi, E_, D_, ALU.mult, ALU.add))
                step.link(v.scalar_tensor_tensor(den[:], xj, H_, den[:], ALU.mult, ALU.add))
                step.link(v.reciprocal(den[:], den[:]))
                step.link(v.tensor_tensor(num[:], xi, bcast(wts[:].unsqueeze(2), [P, B, FEAT]), ALU.mult))
                step.link(v.tensor_tensor(num[:], num[:], xj, ALU.mult))
                return v.tensor_tensor(env["msg"][:, b], num[:], den[:], ALU.mult)

            scatter_pass("l2", [(t_mix, src_i, FEAT), (t_mix, dst_i, FEAT)], key_src, FEAT, acc5, l2_messages, 5)

        v_dst = sb("v_dst", [P, C])

        def d7_alloc(tmp):
            return dict(agg=tmp("agg", [P, 2, WIDE, FEAT]), u=tmp("u", [P, 2, WIDE, FEAT]), dot=tmp("dot", [P, WIDE, FEAT]))

        def d7_prepare(env, step, k, b):
            g, agg, u = nc.gpsimd, env["agg"][:, b], env["u"][:, b]
            a0, a1, h = env["ins"]
            step.link(g.tensor_scalar(u, h[:, b], -1.0 / 5.0, 1.0, ALU.mult, ALU.add))
            step.link(g.tensor_tensor(agg, a0[:, b], a1[:, b], ALU.add))
            step.link(g.tensor_tensor(u, u, h[:, b], ALU.mult))

        def d7_early(dve, env, step, k, b):
            v, u, xc = nc.vector, env["u"][:, b], X[:, bass.ds(k * WIDE, WIDE), :]
            step.link(v.scalar_tensor_tensor(u, env["ins"][2][:, b], -1.0, u, ALU.add, ALU.mult))
            step.link(v.tensor_tensor(xc, xc, env["agg"][:, b], ALU.add))

        def d7_middle(dve, env, step, k, b):
            xc = X[:, bass.ds(k * WIDE, WIDE), :]
            step.link(nc.vector.scalar_tensor_tensor(xc, env["u"][:, b], 0.1, xc, ALU.add, ALU.add))
            dve.sem_inc(env["used_ok"], 1)

        def d7_end(dve, env, step, k, b):
            v, row = nc.vector, env["row"][:, b]
            step.link(ln_back(dve, step, row, env["t"], k))
            step.link(v.tensor_tensor(env["dot"][:], row, bcast(c_row[:, 2:3, :], [P, WIDE, FEAT]), ALU.mult))
            v.tensor_reduce(v_dst[:, bass.ds(k * WIDE, WIDE)], env["dot"][:], AX_X, ALU.add).then_inc(env["row_ok"], 1)

        node_pass("d7", [acc5[0], acc5[1], t_mix], t_last, FEAT, d7_alloc, d7_prepare, 3,
                  (d7_early, d7_middle, none, d7_end), (2, 1 + LN_FRONT, 0, 2 + LN_BACK), QN=WIDE, read=("early_ok",))

        with ExitStack() as ctx:
            attr = sb("attr", [P, T, FEAT], F32, ctx)
            wide_t = sb("wide_t", [P, B, FEAT, FEAT], F32, ctx)
            part = sb("l3_part", [P, B, FEAT], F32, ctx)
            mrow = sb("l3_mrow", [P, B, FEAT], F32, ctx)
            u = sb("l3_u", [P, B], F32, ctx)
            u2 = sb("l3_u2", [P, B], F32, ctx)
            a_s, c_s = semaphore(ctx, "attr_in"), semaphore(ctx, "attr_clear")
            with nc.Block() as block:
                @block.vector
                def _(dve):
                    nc.vector.memset(attr[96:P], 0.0).then_inc(c_s, 1)

                @block.sync
                def _(sp):
                    sp.wait_ge(c_s, 1)
                    sp.dma_start(attr[0:EP], edge_attr_16[0:EP * T].rearrange("(p t) f -> p t f", t=T)).then_inc(a_s, 16)
                    sp.dma_start(attr[EP:EP + 1, 0:EREST], edge_attr_16[EP * T:E].rearrange("(p t) f -> p t f", p=1)
                                 ).then_inc(a_s, 16)
                    sp.wait_ge(a_s, 32)

            def l3_messages(dve, step, env, k, b, gathered):
                v = nc.vector
                h = env["rings"][0][:, b]
                msg = env["msg"]
                v.tensor_scalar(env["pick"][:], env["typs"][:, b], lane[:], None, ALU.is_equal
                                ).then_inc(env["pick_ok"], 1)
                step.link(v.tensor_tensor(part[:], attr[:, bass.ds(k * B, B), :], bcast(c_row[:, 1:2, :], [P, B, FEAT]),
                                          ALU.mult))
                step.link(v.tensor_reduce(u2[:], part[:], AX_X, ALU.add))
                hold(dve, *gathered)
                step.link(v.tensor_tensor(part[:], h, bcast(c_row[:, 0:1, :], [P, B, FEAT]), ALU.mult))
                step.link(v.tensor_reduce(u[:], part[:], AX_X, ALU.add))
                step.link(v.tensor_tensor(u[:], u[:], u2[:], ALU.add))
                hold(dve, env["mats_ok"], k + 1)
                for s in range(B):
                    last = v.tensor_tensor(wide_t[:, s], env["ps_mid"][:, 256 * s:256 * (s + 1)].rearrange(
                        "p (i o) -> p i o", o=FEAT), bcast(h[:, s].unsqueeze(2), [P, FEAT, FEAT]), ALU.mult)
                step.link(last)
                step.link(v.tensor_reduce(mrow[:], wide_t[:].rearrange("p s i o -> p s o i"), AX_X, ALU.add))
                v.tensor_copy(msg[:, b, :, FEAT:2 * FEAT], mrow[:])
                return v.tensor_tensor(msg[:, b, :, 0:FEAT], mrow[:], bcast(u[:].unsqueeze(2), [P, B, FEAT]), ALU.mult)

            scatter_pass("l3", [(t_last, src_i, FEAT)], key_dst, 2 * FEAT, acc6, l3_messages, 7, extra=True)

        def d8_alloc(tmp):
            return dict(agg=tmp("agg", [P, 2, WIDE, 2 * FEAT]), u=tmp("u", [P, WIDE, FEAT]))

        def d8_prepare(env, step, k, b):
            a0, a1 = env["ins"]
            step.link(nc.gpsimd.tensor_tensor(env["agg"][:, b], a0[:, b], a1[:, b], ALU.add))

        def d8_middle(dve, env, step, k, b):
            v, agg, u, cols = nc.vector, env["agg"][:, b], env["u"], bass.ds(k * WIDE, WIDE)
            step.link(v.tensor_tensor(u[:], agg[:, :, FEAT:2 * FEAT], bcast(v_dst[:, cols].unsqueeze(2), [P, WIDE, FEAT]),
                                      ALU.mult))
            step.link(v.tensor_tensor(u[:], u[:], agg[:, :, 0:FEAT], ALU.add))
            step.link(v.tensor_tensor(X[:, cols, :], X[:, cols, :], u[:], ALU.add))
            dve.sem_inc(env["used_ok"], 1)
            dve.sem_inc(env["row_ok"], 1)

        node_pass("d8", [acc6[0], acc6[1]], None, FEAT, d8_alloc, d8_prepare, 1, (none, d8_middle, none, none),
                  (0, 3, 0, 0), norm=False, QN=WIDE,
                  store=lambda k, b: (out.rearrange("(p c) f -> p c f", c=C)[:, bass.ds(k * WIDE, WIDE), :],
                                      X[0:NPART, bass.ds(k * WIDE, WIDE), :]))


INPUTS = ["x", "src", "dst", "edge_attr_16", "edge_type_8", "edge_type_90", "edge_weight",
          "L0_gnn_W1", "L0_gnn_a_src1", "L0_gnn_a_dst1", "L0_gnn_b1", "L0_gnn_W2", "L0_gnn_a_src2", "L0_gnn_a_dst2",
          "L0_gnn_b2", "L0_gnn_Wf", "L0_gnn_bf", "L1_gnn_W1", "L1_gnn_root1", "L1_gnn_b1", "L1_gnn_W2",
          "L1_gnn_root2", "L1_gnn_b2", "L3_gnn_Ws", "L3_gnn_Wa", "L3_gnn_weight", "L3_gnn_w_comp"]


def kernel(**inputs):
    import numpy as np
    import concourse.bacc as bacc
    from concourse.bass_utils import run_bass_kernel_spmd

    nc = bacc.Bacc("TRN2", target_bir_lowering=False, num_devices=1)
    arrays, args = {}, []
    for name in INPUTS:
        a = np.ascontiguousarray(inputs[name])
        arrays[f"in_{name}"] = a
        args.append(nc.dram_tensor(f"in_{name}", a.shape, mybir.dt.from_np(a.dtype), kind="ExternalInput").ap())
    shape = inputs["x"].shape
    args.append(nc.dram_tensor("out_0", tuple(shape), F32, kind="ExternalOutput").ap())
    gnn_kernel(nc, *args)
    r = run_bass_kernel_spmd(nc, [arrays], core_ids=[0])
    return r.results[0]["out_0"]
```
